# Optimizing a Trainium2 kernel written in Bass

```python
import numpy as np
import jax
import jax.numpy as jnp

def _softmax(x, axis=-1):
    return jax.nn.softmax(x, axis=axis)

def _gelu(x):
    return jax.nn.gelu(x, approximate=True)

def _silu(x):
    return jax.nn.silu(x)

def _sigmoid(x):
    return jax.nn.sigmoid(x)

def _layernorm(x, axis=-1, eps=1e-05):
    m = jnp.mean(x, axis=axis, keepdims=True)
    v = jnp.var(x, axis=axis, keepdims=True)
    return (x - m) / jnp.sqrt(v + eps)

def _scatter_add(tgt, idx, src, axis=0):
    return tgt.at[idx].add(src)

def _segment_sum(src, seg, n):
    return jax.ops.segment_sum(src, seg, n)
kernel_name = 'mk_audio_tower_d1_tok_audfeat1024_r4_892d62'

def setup_inputs(seed: int=0):
    np.random.seed(seed)
    _w = jnp.asarray

    def _rec_inputs():
        import jax
        import jax.numpy as jnp
        _rk = jax.random.key(seed)
        x = 7.22013e-05 + 1.00017 * jax.random.normal(jax.random.fold_in(_rk, 1), (128, 256, 8), jnp.float32)
        return x
    x = _rec_inputs()

    def _L0_tok_setup():
        import jax, jax.numpy as jnp
        import numpy as np
        B, S, C_IN = (128, 2048, 8)
        PERIOD, N_FILTERS, D_MODEL = (16, 64, 256)
        key = jax.random.key(seed)
        k1, k2, k3, k4 = jax.random.split(key, 4)
        x = jax.random.normal(k1, (B, S, C_IN), dtype=jnp.float32)
        conv_w = jax.random.normal(k2, (C_IN, N_FILTERS, PERIOD), dtype=jnp.float32) * (1.0 / np.sqrt(PERIOD))
        fan_in = N_FILTERS * C_IN
        emb_w = jax.random.normal(k3, (D_MODEL, fan_in), dtype=jnp.float32) * (1.0 / np.sqrt(fan_in))
        emb_b = jax.random.normal(k4, (D_MODEL,), dtype=jnp.float32) * 0.01
        return {'x': x, 'conv_w': conv_w, 'emb_w': emb_w, 'emb_b': emb_b}
    _L0_tok_all = _L0_tok_setup()
    _L0_tok_in = {k: v for k, v in _L0_tok_all.items() if k in ('conv_w', 'emb_w', 'emb_b')}
    del _L0_tok_all

    def _L0_attn_setup():
        import jax, jax.numpy as jnp
        import numpy as np
        DIM = 256
        HEADS = 16
        DIM_HEAD = DIM // HEADS
        LATENT = DIM // 4
        SCALE = DIM_HEAD ** (-0.5)
        key = jax.random.key(seed)
        ks = jax.random.split(key, 8)
        B, S = (2, 512)
        init = lambda k, shape, fan_in: jax.random.normal(k, shape, jnp.float32) * fan_in ** (-0.5)
        return {'x': jax.random.normal(ks[0], (B, S, DIM), jnp.float32), 'Wq': init(ks[1], (DIM, DIM), DIM), 'bq': jnp.zeros((DIM,), jnp.float32), 'Wl': init(ks[2], (DIM, LATENT), DIM), 'bl': jnp.zeros((LATENT,), jnp.float32), 'Wk': init(ks[3], (LATENT, DIM), LATENT), 'bk': jnp.zeros((DIM,), jnp.float32), 'Wv': init(ks[4], (LATENT, DIM), LATENT), 'bv': jnp.zeros((DIM,), jnp.float32), 'Wo': init(ks[5], (DIM, DIM), DIM), 'bo': jnp.zeros((DIM,), jnp.float32)}
    _L0_attn_all = _L0_attn_setup()
    _L0_attn_in = {k: v for k, v in _L0_attn_all.items() if k in ('Wq', 'bq', 'Wl', 'bl', 'Wk', 'bk', 'Wv', 'bv', 'Wo', 'bo')}
    del _L0_attn_all

    def _L0_ffn_setup():
        import jax, jax.numpy as jnp
        import numpy as np
        B, S, H = (1, 512, 256)
        E, K = (16, 4)
        G, TG = (4, 2)
        I_MOE = 128
        N_SH = 2
        SCALE = 2.5

        def _mlp(x, gw, uw, dw):
            return jax.nn.silu(x @ gw.T) * (x @ uw.T) @ dw.T

        def _route(x2d, router_weight, e_bias):
            T = x2d.shape[0]
            scores = jax.nn.sigmoid(x2d @ router_weight.T)
            sc = scores + e_bias[None, :]
            group_scores = jnp.sum(jax.lax.top_k(sc.reshape(T, G, E // G), 2)[0], axis=-1)
            _, gidx = jax.lax.top_k(group_scores, TG)
            gmask = jnp.zeros((T, G), sc.dtype).at[jnp.arange(T)[:, None], gidx].set(1.0)
            smask = jnp.repeat(gmask, E // G, axis=1)
            masked = jnp.where(smask > 0, sc, 0.0)
            _, tidx = jax.lax.top_k(masked, K)
            tw = jnp.take_along_axis(scores, tidx, axis=1)
            tw = tw / (jnp.sum(tw, axis=-1, keepdims=True) + 1e-20)
            tw = tw * SCALE
            return (tidx, tw)

        def _moe_forward(hidden_states, router_weight, e_bias, gate_w, up_w, down_w, sh_gate_w, sh_up_w, sh_down_w):
            orig_shape = hidden_states.shape
            x = hidden_states.reshape(-1, H)
            T = x.shape[0]
            tidx, tw = _route(x, router_weight, e_bias)
            g = jnp.einsum('th,eih->tei', x, gate_w)
            u = jnp.einsum('th,eih->tei', x, up_w)
            h = jax.nn.silu(g) * u
            yo = jnp.einsum('tei,ehi->teh', h, down_w)
            combine = jnp.zeros((T, E), tw.dtype).at[jnp.arange(T)[:, None], tidx].add(tw)
            routed = jnp.einsum('te,teh->th', combine, yo)
            shared = _mlp(hidden_states.reshape(-1, H), sh_gate_w, sh_up_w, sh_down_w)
            return (routed + shared).reshape(orig_shape)
        key = jax.random.key(seed)
        ks = jax.random.split(key, 9)
        s = 0.02
        return {'hidden_states': jax.random.normal(ks[0], (B, S, H), jnp.float32), 'router_weight': jax.random.normal(ks[1], (E, H), jnp.float32) * s, 'e_bias': jnp.zeros((E,), jnp.float32), 'gate_w': jax.random.normal(ks[2], (E, I_MOE, H), jnp.float32) * s, 'up_w': jax.random.normal(ks[3], (E, I_MOE, H), jnp.float32) * s, 'down_w': jax.random.normal(ks[4], (E, H, I_MOE), jnp.float32) * s, 'sh_gate_w': jax.random.normal(ks[5], (N_SH * I_MOE, H), jnp.float32) * s, 'sh_up_w': jax.random.normal(ks[6], (N_SH * I_MOE, H), jnp.float32) * s, 'sh_down_w': jax.random.normal(ks[7], (H, N_SH * I_MOE), jnp.float32) * s}
    _L0_ffn_all = _L0_ffn_setup()
    _L0_ffn_in = {k: v for k, v in _L0_ffn_all.items() if k in ('router_weight', 'e_bias', 'gate_w', 'up_w', 'down_w', 'sh_gate_w', 'sh_up_w', 'sh_down_w')}
    del _L0_ffn_all
    return {'x': x, 'L0_tok_conv_w': _L0_tok_in['conv_w'], 'L0_tok_emb_w': _L0_tok_in['emb_w'], 'L0_tok_emb_b': _L0_tok_in['emb_b'], 'L0_attn_Wq': _L0_attn_in['Wq'], 'L0_attn_bq': _L0_attn_in['bq'], 'L0_attn_Wl': _L0_attn_in['Wl'], 'L0_attn_bl': _L0_attn_in['bl'], 'L0_attn_Wk': _L0_attn_in['Wk'], 'L0_attn_bk': _L0_attn_in['bk'], 'L0_attn_Wv': _L0_attn_in['Wv'], 'L0_attn_bv': _L0_attn_in['bv'], 'L0_attn_Wo': _L0_attn_in['Wo'], 'L0_attn_bo': _L0_attn_in['bo'], 'L0_ffn_router_weight': _L0_ffn_in['router_weight'], 'L0_ffn_e_bias': _L0_ffn_in['e_bias'], 'L0_ffn_gate_w': _L0_ffn_in['gate_w'], 'L0_ffn_up_w': _L0_ffn_in['up_w'], 'L0_ffn_down_w': _L0_ffn_in['down_w'], 'L0_ffn_sh_gate_w': _L0_ffn_in['sh_gate_w'], 'L0_ffn_sh_up_w': _L0_ffn_in['sh_up_w'], 'L0_ffn_sh_down_w': _L0_ffn_in['sh_down_w']}

def reference(x, L0_tok_conv_w, L0_tok_emb_w, L0_tok_emb_b, L0_attn_Wq, L0_attn_bq, L0_attn_Wl, L0_attn_bl, L0_attn_Wk, L0_attn_bk, L0_attn_Wv, L0_attn_bv, L0_attn_Wo, L0_attn_bo, L0_ffn_router_weight, L0_ffn_e_bias, L0_ffn_gate_w, L0_ffn_up_w, L0_ffn_down_w, L0_ffn_sh_gate_w, L0_ffn_sh_up_w, L0_ffn_sh_down_w):
    import jax
    import jax.numpy as jnp

    def _L0_tok_ref(x, conv_w, emb_w, emb_b):
        import jax, jax.numpy as jnp
        import numpy as np
        B, S, C_IN = (128, 2048, 8)
        PERIOD, N_FILTERS, D_MODEL = (16, 64, 256)
        b, s, c = x.shape
        nf, p = (conv_w.shape[1], conv_w.shape[2])
        l = s // p
        patches = x.reshape(b, l, p, c)
        feat = jnp.einsum('blpc,cfp->blcf', patches, conv_w)
        feat = feat.reshape(b, l, c * nf)
        y = jnp.einsum('blk,dk->bld', feat, emb_w) + emb_b
        return jax.nn.relu(y)

    def _L0_attn_ref(x, Wq, bq, Wl, bl, Wk, bk, Wv, bv, Wo, bo):
        import jax, jax.numpy as jnp
        import numpy as np
        DIM = 256
        HEADS = 16
        DIM_HEAD = DIM // HEADS
        LATENT = DIM // 4
        SCALE = DIM_HEAD ** (-0.5)
        B, S, D = x.shape
        H, Dh = (HEADS, DIM_HEAD)
        q = (x @ Wq + bq).reshape(B, S, H, Dh)
        latent = x @ Wl + bl
        k = (latent @ Wk + bk).reshape(B, S, H, Dh)
        v = (latent @ Wv + bv).reshape(B, S, H, Dh)
        scores = jnp.einsum('bihd,bjhd->bhij', q, k) * SCALE
        attn = jax.nn.softmax(scores, axis=-1)
        out = jnp.einsum('bhij,bjhd->bihd', attn, v).reshape(B, S, D)
        out = out @ Wo + bo
        return out

    def _L0_ffn_ref(hidden_states, router_weight, e_bias, gate_w, up_w, down_w, sh_gate_w, sh_up_w, sh_down_w):
        import jax, jax.numpy as jnp
        import numpy as np
        B, S, H = (1, 512, 256)
        E, K = (16, 4)
        G, TG = (4, 2)
        I_MOE = 128
        N_SH = 2
        SCALE = 2.5

        def _mlp(x, gw, uw, dw):
            return jax.nn.silu(x @ gw.T) * (x @ uw.T) @ dw.T

        def _route(x2d, router_weight, e_bias):
            T = x2d.shape[0]
            scores = jax.nn.sigmoid(x2d @ router_weight.T)
            sc = scores + e_bias[None, :]
            group_scores = jnp.sum(jax.lax.top_k(sc.reshape(T, G, E // G), 2)[0], axis=-1)
            _, gidx = jax.lax.top_k(group_scores, TG)
            gmask = jnp.zeros((T, G), sc.dtype).at[jnp.arange(T)[:, None], gidx].set(1.0)
            smask = jnp.repeat(gmask, E // G, axis=1)
            masked = jnp.where(smask > 0, sc, 0.0)
            _, tidx = jax.lax.top_k(masked, K)
            tw = jnp.take_along_axis(scores, tidx, axis=1)
            tw = tw / (jnp.sum(tw, axis=-1, keepdims=True) + 1e-20)
            tw = tw * SCALE
            return (tidx, tw)

        def _moe_forward(hidden_states, router_weight, e_bias, gate_w, up_w, down_w, sh_gate_w, sh_up_w, sh_down_w):
            orig_shape = hidden_states.shape
            x = hidden_states.reshape(-1, H)
            T = x.shape[0]
            tidx, tw = _route(x, router_weight, e_bias)
            g = jnp.einsum('th,eih->tei', x, gate_w)
            u = jnp.einsum('th,eih->tei', x, up_w)
            h = jax.nn.silu(g) * u
            yo = jnp.einsum('tei,ehi->teh', h, down_w)
            combine = jnp.zeros((T, E), tw.dtype).at[jnp.arange(T)[:, None], tidx].add(tw)
            routed = jnp.einsum('te,teh->th', combine, yo)
            shared = _mlp(hidden_states.reshape(-1, H), sh_gate_w, sh_up_w, sh_down_w)
            return (routed + shared).reshape(orig_shape)
        return _moe_forward(hidden_states, router_weight, e_bias, gate_w, up_w, down_w, sh_gate_w, sh_up_w, sh_down_w)
    h = _L0_tok_ref(x, L0_tok_conv_w, L0_tok_emb_w, L0_tok_emb_b)
    h = h + _L0_attn_ref(_layernorm(h, axis=-1), L0_attn_Wq, L0_attn_bq, L0_attn_Wl, L0_attn_bl, L0_attn_Wk, L0_attn_bk, L0_attn_Wv, L0_attn_bv, L0_attn_Wo, L0_attn_bo)
    h = h + _L0_ffn_ref(_layernorm(h, axis=-1), L0_ffn_router_weight, L0_ffn_e_bias, L0_ffn_gate_w, L0_ffn_up_w, L0_ffn_down_w, L0_ffn_sh_gate_w, L0_ffn_sh_up_w, L0_ffn_sh_down_w)
    return h

_drawn_inputs = setup_inputs


def setup_inputs(seed=0):
    import zlib

    import numpy as np

    out = dict(_drawn_inputs(seed))
    spreads = {'L0_attn_bq': (0.0, 0.1),
     'L0_attn_bl': (0.0, 0.1),
     'L0_attn_bk': (0.0, 2.0),
     'L0_attn_bv': (0.0, 0.1),
     'L0_attn_bo': (0.0, 0.1),
     'L0_ffn_e_bias': (0.0, 0.396)}
    factors = {'L0_tok_emb_b': 4.144,
     'L0_ffn_router_weight': 6.527,
     'L0_ffn_gate_w': 3.109,
     'L0_ffn_up_w': 3.096,
     'L0_ffn_down_w': 3.1,
     'L0_ffn_sh_gate_w': 3.1,
     'L0_ffn_sh_up_w': 2.864,
     'L0_ffn_sh_down_w': 2.835}
    for name, (base, spread) in spreads.items():
        noise = np.random.default_rng([zlib.crc32(name.encode()), seed]).standard_normal(out[name].shape)
        drawn = base * np.exp(spread * noise) if base else spread * noise
        out[name] = jnp.asarray(drawn.astype(out[name].dtype))
    for name, factor in factors.items():
        out[name] = (out[name] * factor).astype(out[name].dtype)
    return out
```

```python
from contextlib import ExitStack

import concourse.bass as bass
from concourse import mybir

F32 = mybir.dt.float32
F32R = mybir.dt.float32r
ALU = mybir.AluOpType
ACT = mybir.ActivationFunctionType
AX_X = mybir.AxisListType.X

P = 128
TOK = 2048
SEQ = 16
D = 256
KD = D // P
CH = 512
NCH = TOK // CH
NT = CH // P
Q = 32
NQ = P // Q
NB = 2 * NQ * NT * 2
NE = 16
NSH = 2
NU = NE + NSH
NGRP, TOPG, TOPK = 4, 2, 4
EPG = NE // NGRP
SCALE = 16 ** -0.5
ROUTE_SCALE = 2.5
EPS = 1e-5

C_BQ, C_BL, C_BK, C_BV, C_EVEN, C_ODD, NCOL = 0, 2, 3, 5, 7, 8, 9
W_Q, W_L, W_K, W_V, W_O, W_R, W_END = 0, 512, 768, 1024, 1280, 1792, 1824
STEPS = 17
ROUTE_OPS = 25


def tower(nc, x_t, tok_w, attn_w, ffn_w, cols, rows, tri, ident, out_t):
    at = {"end": (nc.sbuf_base + 63) // 64 * 64}

    def sb(name, shape, dt=F32, over=None):
        size = 4
        for n in shape[1:]:
            size *= n
        start = at[over] if over else at["end"]
        at[name] = start
        if not over:
            at["end"] += (size + 31) // 32 * 32
        assert start + size <= nc.sbuf_usable_end, (name, start, size)
        return nc.alloc_sbuf_tensor_at(name, shape, dt, offset=start)

    with ExitStack() as ctx:
        def sem(name):
            return ctx.enter_context(nc.semaphore(name))

        def pair(name):
            return sem(name + "0"), sem(name + "1")

        def psum(name, shape):
            return ctx.enter_context(nc.psum_tensor(name, shape, F32))

        ffn_h = sb("ffn_h", [P, NU, 3 * D], F32R)
        ffn_l = sb("ffn_l", [P, NU, 3 * D], F32R)
        aw_h = sb("aw_h", [P, W_R], F32R)
        aw_l = sb("aw_l", [P, W_R], F32R)
        rw_hl = sb("rw_hl", [P, KD, P], F32R)
        rw_h = sb("rw_h", [P, KD, P], F32R)
        w_tok = sb("w_tok", [P, D])
        ident_s = sb("ident_s", [P, P])
        pick = sb("pick", [2 * NE, NE], F32R)
        col = sb("col", [P, NCOL])
        bq_s = sb("bq_s", [P, KD])
        bk_e = sb("bk_e", [P, KD])
        row = sb("row", [P, 2 * D + NE])
        tri_s = sb("tri_s", [P, NE * NE + NGRP * NGRP])
        even, odd = col[:, C_EVEN:C_EVEN + 1], col[:, C_ODD:C_ODD + 1]

        x_s = sb("x_s", [P, CH])
        hres = sb("hres", [P, NT, D])
        q_t = sb("q_t", [P, KD, CH])
        out_s = sb("out_s", [P, KD, CH], over="q_t")
        s1 = sb("s1", [P, CH], F32R)
        v_s = sb("v_s", [P, NT, D])
        xn = sb("xn", [P, NT, D])
        sd = sb("sd", [P, NB, SEQ], over="xn")
        of = sb("of", [P, KD, CH], over="xn")
        keo = sb("keo", [P, KD, 2, CH])
        pt = sb("pt", [P, NB, Q], over="keo")
        cmp = sb("cmp", [P, 2, NT * NE * NE], over="keo")
        emb_s = sb("emb_s", [P, 4 * (D + Q)], over="keo")
        xnt = sb("xnt", [P, 2, KD, CH], F32R)
        oht = sb("oht", [P, 2, KD, CH], F32R, over="xnt")
        p32 = sb("p32", [P, NB, Q], over="xnt")
        tmp = sb("tmp", [P, CH])
        xn2 = sb("xn2", [P, 2, 2, KD, CH], F32R)
        comb_t = sb("comb_t", [2 * NE, 2, CH], F32R)
        comb_hl = sb("comb_hl", [P, NT, 2 * NE], F32R)
        bn = sb("bn", [P, NT, 6])
        mv = sb("mv", [P, NT, 2])
        rstd = sb("rstd", [P, 4, NT])
        mx = sb("mx", [P, NB])
        rc = sb("rc", [P, 3, NB])
        rt = sb("rt", [P, 4, NT * NE])
        rg = sb("rg", [P, 10, NT * NGRP])
        sg = sb("sg", [P, CH])
        h_s = sb("h_s", [P, 2, CH])
        hh = sb("hh", [P, 2, CH], F32R)
        hl = sb("hl", [P, 2, CH], F32R)
        aw_s = sb("aw_s", [P, W_END], over="h_s")
        at["stage"] = at["xn2"] + 2 * KD * CH * 4
        stage = sb("stage", [P, 2, 3 * D], over="stage")

        pre = psum("pre", [P, 3, 512])
        pg = psum("pg", [P, 512])
        pu = psum("pu", [P, 512])
        pw = psum("pw", [P, 512])
        po = psum("po", [P, KD, 512])
        pre_tok = pre[:, 0:2, :].rearrange("p b (t d) -> p (b t) d", d=D)
        pre_blk = pre[:, 0:2, :].rearrange("p b (n j) -> p (b n) j", j=Q)

        tok_in, small_in, aw_in, x_in = sem("tok_in"), sem("small_in"), sem("aw_in"), sem("x_in")
        ffn_in = [sem("ffn_in0"), sem("ffn_in1")]
        consts, wtok_mm, wtok_done = sem("consts"), sem("wtok_mm"), sem("wtok_done")
        aw_h_done, aw_l_done, rw_done = sem("aw_h_done"), sem("aw_l_done"), sem("rw_done")
        fw_h_done, fw_l_done = sem("fw_h_done"), sem("fw_l_done")
        h0_mm, h0_sum, h0_done, h0_bo = sem("h0_mm"), sem("h0_sum"), sem("h0_done"), sem("h0_bo")
        ln_bn, ln_mv, ln_var, ln_rs, ln_xn = (pair(x) for x in ("ln_bn", "ln_mv", "ln_var", "ln_rs", "ln_xn"))
        xn_tr, xn_hi, xn_lo = pair("xn_tr"), pair("xn_hi"), pair("xn_lo")
        q_mm, q_done, lat_mm, lat_f, lat_h, lat_l = (sem(x) for x in ("q_mm", "q_done", "lat_mm", "lat_f", "lat_h", "lat_l"))
        v_mm, v_done = sem("v_mm"), sem("v_done")
        k_mm, k_even, k_odd = pair("k_mm"), pair("k_even"), pair("k_odd")
        sc_mm, sc_t, sc_done = pair("sc_mm"), pair("sc_t"), pair("sc_done")
        sc_row, pv_row = (pair("sc_row0"), pair("sc_row1")), (pair("pv_row0"), pair("pv_row1"))
        sm_max, sm_sub, sm_exp, sm_sum, sm_rc, sm_r01 = (sem(x) for x in ("sm_max", "sm_sub", "sm_exp", "sm_sum", "sm_rc", "sm_r01"))
        p_even, p_odd, pt_done = sem("p_even"), sem("p_odd"), sem("pt_done")
        pv_mm, pv_t, o_done, o_hi, o_lo = (pair(x) for x in ("pv_mm", "pv_t", "o_done", "o_hi", "o_lo"))
        wo_mm, h1_done = sem("wo_mm"), sem("h1_done")
        lg_mm, lg_sb, lg_tr, lg_tok, lg_exp = (sem(x) for x in ("lg_mm", "lg_sb", "lg_tr", "lg_tok", "lg_exp"))
        route = sem("route")
        comb_tr, comb_done = sem("comb_tr"), sem("comb_done")
        res_mm = sem("res_mm")
        g_mm, u_mm = sem("g_mm"), sem("u_mm")
        silu, gated, weighted, h_hi, h_lo = sem("silu"), sem("gated"), sem("weighted"), sem("h_hi"), sem("h_lo")
        w_mm, down = sem("w_mm"), sem("down")
        po_free = sem("po_free")
        out_sb, stored = sem("out_sb"), sem("stored")

        block = ctx.enter_context(nc.Block())

        def par(c):
            return c % 2

        def bc(ap, n):
            return ap.unsqueeze(len(ap.shape)).to_broadcast([*ap.shape, n])

        def value(eng, n):
            return n if isinstance(n, int) else eng.snap(n)

        def grouped(ap):
            return ap.rearrange("p (b t n) -> p b t n", b=NQ, t=NT)

        def by_group(ap):
            return ap.rearrange("p (t b n) -> p b t n", b=NQ, t=NT)

        @block.sync
        def _(sp):
            def load_expert(u):
                if u >= 2:
                    sp.wait_ge(fw_h_done, u - 1)
                    sp.wait_ge(fw_l_done, u - 1)
                sp.dma_start(stage[:, u % 2, :], ffn_w[u]).then_inc(ffn_in[u % 2], 16)

            def load_x(c, first=False):
                if not first:
                    sp.wait_ge(h0_mm, c)
                sp.dma_start(x_s[:, :], x_t[:, bass.ds(c * CH, CH)]).then_inc(x_in, 16)

            def store(c):
                sp.wait_ge(out_sb, c + 1)
                sp.dma_start(out_t[:, :, bass.ds(c * CH, CH)], out_s[:, :, :]).then_inc(stored, 16)

            sp.dma_start(emb_s[:, :], tok_w).then_inc(tok_in, 16)
            load_x(0, first=True)
            sp.dma_start(col[:, :], cols).then_inc(small_in, 16)
            sp.dma_start(row[:, :], rows).then_inc(small_in, 16)
            sp.dma_start(ident_s[:, :], ident).then_inc(small_in, 16)
            sp.dma_start(tri_s[:, :], tri).then_inc(small_in, 16)
            sp.dma_start(aw_s[:, :], attn_w).then_inc(aw_in, 16)
            for u in range(NU):
                load_expert(u)
            with sp.Fori(0, NCH - 1) as c:
                load_x(c + 1)
                store(c)
            store(NCH - 1)
            sp.wait_ge(stored, 16 * NCH)

        @block.tensor
        def _(pe):
            def split_mm(out, w, x, w_cols, x_cols, start, stop):
                n = len(w_cols) * 3
                i = 0
                for wc, xc in zip(w_cols, x_cols):
                    for a, b in ((0, 0), (0, 1), (1, 0)):
                        last = pe.matmul(out, w[a](wc), x[b](xc), start=start and i == 0, stop=stop and i == n - 1)
                        i += 1
                return last

            def transpose_xn(i):
                for k in range(KD):
                    for t in range(NT):
                        last = pe.transpose(pre[:, k, t * P:(t + 1) * P], xn[:, t, k * P:(k + 1) * P], ident_s[:, :])
                last.then_inc(xn_tr[i], 1)

            def prefix(s, c, first=False):
                if s == 0:
                    pe.wait_ge(x_in, 16 * c + 16)
                    if not first:
                        pe.wait_ge(xn_hi[1], c)
                        pe.wait_ge(xn_lo[1], c)
                    for t in range(NT):
                        last = pe.matmul(pre_tok[:, t, :], x_s[:, t * P:(t + 1) * P], w_tok[:, :], start=True, stop=True)
                    last.then_inc(h0_mm, 1)
                if s == 1:
                    pe.wait_ge(ln_xn[0], c + 1)
                    transpose_xn(0)
                if s == 2:
                    pe.wait_ge(xn_hi[0], c + 1)
                    pe.wait_ge(xn_lo[0], c + 1)
                    x = [lambda k, i=i: xnt[:, i, k, :] for i in range(2)]
                    for m in range(KD):
                        w = [lambda k, a=a, m=m: a[:, W_Q + k * D + m * P:W_Q + k * D + m * P + P] for a in (aw_h, aw_l)]
                        last = split_mm(pre[:, m, :], w, x, range(KD), range(KD), True, True)
                    last.then_inc(q_mm, 1)
                    w = [lambda k, a=a: a[:, W_L + k * P:W_L + k * P + P] for a in (aw_h, aw_l)]
                    split_mm(pre[:, 2, :], w, x, range(KD), range(KD), True, True).then_inc(lat_mm, 1)
                if s == 3:
                    pe.wait_ge(lat_l, c + 1)
                    k_half(c, 0)
                    pe.wait_ge(q_done, c + 1)
                    for t in range(NT):
                        for i, w in enumerate((aw_h, aw_l)):
                            last = pe.matmul(pre_tok[:, t, :], s1[:, t * P:(t + 1) * P], w[:, W_V:W_V + D], start=i == 0, stop=i == 1)
                    last.then_inc(v_mm, 1)
                if s == 4:
                    pe.wait_ge(k_even[0], c + 1)
                    pe.wait_ge(k_odd[0], c + 1)
                    k_half(c, 1)
                if s in (5, 6):
                    m = s - 5
                    n = value(pe, c + 1)
                    pe.wait_ge(tok_in, 16)
                    pe.wait_ge(k_even[m], n)
                    pe.wait_ge(k_odd[m], n)
                    pe.wait_ge(v_done if m == 0 else sc_done[0], n)
                    out = pre[:, 0:2, :].rearrange("p b (g t n) -> p (b g) t n", g=2, t=NT)
                    for g in (0, 2, 1, 3):
                        if g % 2:
                            pe.wait_ge(tok_in, 16)
                            pe.wait_ge(sc_row[m][g // 2], n)
                        rows_g = slice(g * Q, g * Q + Q)
                        for t in range(NT):
                            for b in range(NQ):
                                tok = slice(t * P + b * Q, t * P + b * Q + Q)
                                last = pe.matmul(out[b * Q:b * Q + Q, g, t, :], q_t[rows_g, m, tok], keo[rows_g, m, :, tok],
                                                 start=True, stop=True, tile_position=(g * Q, b * Q))
                        if g % 2 == 0:
                            last.then_inc(sc_row[m][g // 2], 1)
                    last.then_inc(sc_mm[m], 1)
                if s in (8, 9):
                    m = s - 8
                    n = value(pe, c + 1)
                    pe.wait_ge(tok_in, 16)
                    pe.wait_ge(pt_done if m == 0 else o_done[0], n)
                    out = pre[:, 0:2, :].rearrange("p b (g t n) -> p (b g) t n", g=2, t=NT)
                    for b in (0, 2, 1, 3):
                        if b % 2:
                            pe.wait_ge(tok_in, 16)
                            pe.wait_ge(pv_row[m][b // 2], n)
                        rows_b = slice(b * Q, b * Q + Q)
                        for t in range(NT):
                            for g in range(NQ):
                                blk = ((m * NQ + g) * NT + t) * 2
                                last = pe.matmul(out[g * Q:g * Q + Q, b, t, :], v_s[rows_b, t, m * P + g * Q:m * P + g * Q + Q],
                                                 pt[rows_b, blk:blk + 2, :], start=True, stop=True, tile_position=(b * Q, g * Q))
                        if b % 2 == 0:
                            last.then_inc(pv_row[m][b // 2], 1)
                    last.then_inc(pv_mm[m], 1)
                if s == 10:
                    for m in range(KD):
                        pe.wait_ge(o_hi[m], c + 1)
                        pe.wait_ge(o_lo[m], c + 1)
                    for t in range(NT):
                        o = [lambda m, i=i, t=t: oht[:, i, m, t * P:(t + 1) * P] for i in range(2)]
                        w = [lambda m, a=a: a[:, W_O + m * D:W_O + m * D + D] for a in (aw_h, aw_l)]
                        i = 0
                        for m in range(KD):
                            for a, b in ((0, 0), (0, 1), (1, 0)):
                                last = pe.matmul(pre_tok[:, t, :], o[b](m), w[a](m), start=i == 0, stop=i == 5)
                                i += 1
                    last.then_inc(wo_mm, 1)
                if s == 12:
                    pe.wait_ge(ln_xn[1], c + 1)
                    transpose_xn(1)
                if s == 13:
                    pe.wait_ge(xn_hi[1], c + 1)
                    pe.wait_ge(xn_lo[1], c + 1)
                    pe.wait_ge(rw_done, 1)
                    for k in range(KD):
                        pe.matmul(pre[:, 2, :], rw_hl[:, k, :], xn2[:, par(c), 0, k, :], start=k == 0, stop=False)
                    for k in range(KD):
                        last = pe.matmul(pre[:, 2, :], rw_h[:, k, :], xn2[:, par(c), 1, k, :], start=False, stop=k == KD - 1)
                    last.then_inc(lg_mm, 1)
                if s == 14:
                    n = value(pe, c + 1)
                    pe.wait_ge(tok_in, 16)
                    pe.wait_ge(lg_sb, n)
                    for t in range(NT):
                        last = pe.transpose(pre[:, 2, t * 32:t * 32 + 32], tmp[0:32, t * P:(t + 1) * P], ident_s[0:32, 0:32])
                    last.then_inc(lg_tr, 1)
                if s == 16:
                    n = value(pe, ROUTE_OPS * (c + 1))
                    pe.wait_ge(tok_in, 16)
                    pe.wait_ge(route, n)
                    for t in range(NT):
                        last = pe.transpose(pre[0:32, 2, t * P:(t + 1) * P], comb_hl[:, t, :].bitcast(F32), ident_s[:, :])
                    last.then_inc(comb_tr, 1)

            def k_half(c, m):
                for i, w in enumerate((aw_h, aw_l)):
                    last = pe.matmul(pre[:, 2, :], w[:, W_K + m * P:W_K + m * P + P], s1[:, :], start=i == 0, stop=i == 1)
                last.then_inc(k_mm[m], 1)

            def residual(c):
                pe.wait_ge(po_free, c + 1)
                pe.wait_ge(h1_done, c + 1)
                for k in range(KD):
                    for t in range(NT):
                        last = pe.matmul(po[:, k, t * P:(t + 1) * P], hres[:, t, k * P:(k + 1) * P], ident_s[:, :],
                                         is_transpose=True, start=t == 0, stop=False, skip_group_check=True)
                last.then_inc(res_mm, 1)

            def ffn_mm(c, u, out, off):
                i = 0
                for k in range(KD):
                    for w, part in ((ffn_h, 0), (ffn_h, 1), (ffn_l, 0)):
                        last = pe.matmul(out, w[:, u, off + k * P:off + k * P + P], xn2[:, par(c), part, k, :],
                                         start=i == 0, stop=i == 5)
                        i += 1
                return last

            def expert(c, u, first=False):
                if first:
                    pe.wait_ge(fw_l_done, u + 1)
                    pe.wait_ge(fw_h_done, u + 1)
                if u > 0:
                    pe.wait_ge(silu, c * NU + u)
                ffn_mm(c, u, pg[:, :], 0).then_inc(g_mm, 1)
                if u > 0:
                    pe.wait_ge(gated, c * NU + u)
                ffn_mm(c, u, pu[:, :], D).then_inc(u_mm, 1)
                if u >= NSH:
                    e = u - NSH
                    n = value(pe, c + 1 if e == 0 else c * NU + u)
                    pe.wait_ge(small_in, 64)
                    pe.wait_ge(comb_done if e == 0 else weighted, n)
                    pe.matmul(pw[:, :], pick[:, e:e + 1].to_broadcast([2 * NE, P]), comb_t[:, par(c), :],
                              start=True, stop=True).then_inc(w_mm, 1)
                if u > 0:
                    down_mm(c, u - 1)

            def down_mm(c, u):
                pe.wait_ge(h_hi, c * NU + u + 1)
                pe.wait_ge(h_lo, c * NU + u + 1)
                for k in range(KD):
                    for i, (w, x) in enumerate(((ffn_h, hh), (ffn_h, hl), (ffn_l, hh))):
                        last = pe.matmul(po[:, k, :], w[:, u, 2 * D + k * P:2 * D + k * P + P], x[:, u % 2, :],
                                         start=False, stop=u == NU - 1 and i == 2, skip_group_check=True)
                last.then_inc(down, 1)

            pe.wait_ge(tok_in, 16)
            for i in range(4):
                last = pe.matmul(pre[i * Q:i * Q + Q, 0, 0:D], emb_s[:, 4 * D + i * Q:4 * D + i * Q + Q], emb_s[:, i * D:i * D + D],
                                 start=True, stop=True)
            last.then_inc(wtok_mm, 1)
            pe.wait_ge(wtok_done, 1)
            pe.wait_ge(small_in, 64)
            for s in range(STEPS):
                if s == 2:
                    pe.wait_ge(aw_h_done, 1)
                    pe.wait_ge(aw_l_done, 1)
                prefix(s, 0, first=True)
            residual(0)
            for u in range(NU):
                expert(0, u, first=True)
            down_mm(0, NU - 1)
            for s in range(STEPS):
                prefix(s, 1)
            with pe.Fori(1, NCH - 1) as c:
                residual(c)
                for u in range(NU):
                    expert(c, u)
                down_mm(c, NU - 1)
                for s in range(STEPS):
                    prefix(s, c + 1)
            residual(NCH - 1)
            for u in range(NU):
                expert(NCH - 1, u)
            down_mm(NCH - 1, NU - 1)

        @block.scalar
        def _(act):
            def prefix(s, c, first=False):
                if s in (1, 12):
                    i = int(s == 12)
                    act.wait_ge(xn_tr[i], c + 1)
                    dst = xnt[:, 0, :, :] if i == 0 else xn2[:, par(c), 0, :, :]
                    act.activation(dst, pre[:, 0:2, :], ACT.Copy).then_inc(xn_hi[i], 1)
                if s == 2:
                    act.wait_ge(q_mm, c + 1)
                    if not first:
                        act.wait_ge(stored, 16 * c)
                    for m in range(KD):
                        last = act.activation(q_t[:, m, :], pre[:, m, :], ACT.Identity, bias=bq_s[:, m:m + 1], scale=SCALE)
                    last.then_inc(q_done, 1)
                    act.wait_ge(lat_f, c + 1)
                    act.activation(s1[:, :], tmp[:, :], ACT.Copy).then_inc(lat_h, 1)
                if s == 3:
                    k_even_heads(c, 0)
                    act.wait_ge(v_mm, c + 1)
                    act.activation(v_s[:, :, :], pre_tok, ACT.Copy).then_inc(v_done, 1)
                if s == 4:
                    k_even_heads(c, 1)
                if s in (5, 6):
                    m = s - 5
                    act.wait_ge(sc_mm[m], c + 1)
                    if m == 1:
                        act.wait_ge(sc_done[0], c + 1)
                    act.activation(tmp[:, :].rearrange("p (n j) -> p n j", j=SEQ), pre_blk[:, :, 0:SEQ], ACT.Identity, bias=0.0, scale=even)\
                       .then_inc(sc_t[m], 1)
                if s == 7:
                    act.wait_ge(sm_sub, c + 1)
                    act.activation(sd[:, :, :], sd[:, :, :], ACT.Exp).then_inc(sm_exp, 1)
                if s in (8, 9):
                    m = s - 8
                    act.wait_ge(pv_mm[m], c + 1)
                    if m == 1:
                        act.wait_ge(o_done[0], c + 1)
                    act.activation(tmp[:, :].rearrange("p (n j) -> p n j", j=Q), pre_blk[:, 1::2, :], ACT.Identity,
                                   bias=col[:, C_BV + m:C_BV + m + 1], scale=odd).then_inc(pv_t[m], 1)
                    act.wait_ge(o_done[m], c + 1)
                    act.activation(by_group(oht[:, 0, m, :]), grouped(of[:, m, :]), ACT.Copy).then_inc(o_hi[m], 1)
                if s == 13:
                    act.wait_ge(lg_mm, c + 1)
                    act.activation(tmp[0:32, :], pre[0:32, 2, :], ACT.Copy).then_inc(lg_sb, 1)
                if s == 14:
                    act.wait_ge(lg_tr, c + 1)
                    act.activation(rt[:, 0:2, :].rearrange("p a n -> p (a n)"), pre[:, 2, 0:NT * 32], ACT.Copy).then_inc(lg_tok, 1)
                    act.wait_ge(route, ROUTE_OPS * c + 1)
                    act.activation(rt[:, 3, :], rt[:, 2, :], ACT.Exp, scale=-1.0).then_inc(lg_exp, 1)
                if s == 16:
                    act.wait_ge(comb_tr, c + 1)
                    act.activation(comb_t[:, par(c), :], pre[0:32, 2, :], ACT.Copy).then_inc(comb_done, 1)

            def k_even_heads(c, m):
                act.wait_ge(k_odd[m], c + 1)
                act.activation(keo[:, m, 0, :], pre[:, 2, :], ACT.Identity, bias=bk_e[:, m:m + 1], scale=even).then_inc(k_even[m], 1)

            def expert(c, u):
                act.wait_ge(g_mm, c * NU + u + 1)
                act.activation(sg[:, :], pg[:, :], ACT.Silu).then_inc(silu, 1)
                act.wait_ge(weighted, c * NU + u + 1)
                if u >= 2:
                    act.wait_ge(down, c * NU + u - 1)
                act.activation(hh[:, u % 2, :], h_s[:, u % 2, :], ACT.Copy).then_inc(h_hi, 1)

            def split_high(u):
                act.wait_ge(ffn_in[u % 2], 16 * (u // 2 + 1))
                act.activation(ffn_h[:, u, :], stage[:, u % 2, :], ACT.Copy).then_inc(fw_h_done, 1)

            act.wait_ge(wtok_mm, 1)
            act.activation(w_tok[:, :], pre[:, 0, 0:D], ACT.Copy).then_inc(wtok_done, 1)
            act.wait_ge(aw_in, 16)
            act.activation(aw_h[:, :], aw_s[:, 0:W_R], ACT.Copy).then_inc(aw_h_done, 1)
            for u in range(4):
                split_high(u)
            for s in range(STEPS):
                prefix(s, 0, first=True)
                if s + 4 < NU:
                    split_high(s + 4)
            for u in range(STEPS + 4, NU):
                split_high(u)
            for u in range(NU):
                expert(0, u)
            for s in range(STEPS):
                prefix(s, 1)
            with act.Fori(1, NCH - 1) as c:
                for u in range(NU):
                    expert(c, u)
                for s in range(STEPS):
                    prefix(s, c + 1)
            for u in range(NU):
                expert(NCH - 1, u)

        @block.vector
        def _(dve):
            def norm_stats(i, c):
                for t in range(NT):
                    last = dve.bn_stats(bn[:, t, :], hres[:, t, :])
                last.then_inc(ln_bn[i], 1)
                n = value(dve, c + 1)
                dve.wait_ge(small_in, 64)
                dve.wait_ge(ln_bn[i], n)
                for t in range(NT):
                    last = dve.bn_aggr(mv[:, t, :], bn[:, t, :])
                last.then_inc(ln_mv[i], 1)

            def norm_apply(i, c):
                dve.wait_ge(ln_rs[i], c + 1)
                for t in range(NT):
                    last = dve.tensor_scalar(xn[:, t, :], hres[:, t, :], mv[:, t, 0:1], rstd[:, 2, t:t + 1], ALU.subtract, ALU.mult)
                last.then_inc(ln_xn[i], 1)

            def prefix(s, c, first=False):
                if s == 0:
                    dve.wait_ge(h0_mm, c + 1)
                    if not first:
                        dve.wait_ge(res_mm, c)
                    dve.tensor_tensor(hres[:, :, :], pre_tok, row[:, 0:D].unsqueeze(1).to_broadcast([P, NT, D]), ALU.add).then_inc(h0_sum, 1)
                    dve.wait_ge(h0_sum, c + 1)
                    dve.tensor_scalar(hres[:, :, :], hres[:, :, :], 0.0, None, ALU.max).then_inc(h0_done, 1)
                    dve.wait_ge(h0_done, c + 1)
                    norm_stats(0, c)
                    norm_apply(0, c)
                if s in (1, 12):
                    i = int(s == 12)
                    dve.wait_ge(xn_hi[i], c + 1)
                    hi, lo = (xnt[:, j, :, :] if i == 0 else xn2[:, par(c), j, :, :] for j in range(2))
                    dve.tensor_tensor(lo, pre[:, 0:2, :], hi.bitcast(F32), ALU.subtract).then_inc(xn_lo[i], 1)
                if s == 2:
                    dve.wait_ge(lat_mm, c + 1)
                    dve.tensor_scalar(tmp[:, :], pre[:, 2, :], col[:, C_BL:C_BL + 1], None, ALU.add).then_inc(lat_f, 1)
                    dve.wait_ge(lat_h, c + 1)
                    dve.tensor_tensor(s1[64:128, :], tmp[64:128, :], s1[64:128, :].bitcast(F32), ALU.subtract).then_inc(lat_l, 1)
                if s in (3, 4):
                    m = s - 3
                    dve.wait_ge(k_mm[m], c + 1)
                    dve.tensor_scalar(keo[:, m, 1, :], pre[:, 2, :], col[:, C_BK + m:C_BK + m + 1], odd, ALU.add, ALU.mult).then_inc(k_odd[m], 1)
                if s in (5, 6):
                    m = s - 5
                    dve.wait_ge(sc_t[m], c + 1)
                    dve.scalar_tensor_tensor(sd[:, m * 32:m * 32 + 32, :], pre_blk[:, :, SEQ:Q], odd,
                                             tmp[:, :].rearrange("p (n j) -> p n j", j=SEQ), ALU.mult, ALU.add).then_inc(sc_done[m], 1)
                if s == 7:
                    dve.wait_ge(sc_done[0], c + 1)
                    dve.wait_ge(sc_done[1], c + 1)
                    dve.tensor_reduce(mx[:, :], sd[:, :, :], AX_X, ALU.max).then_inc(sm_max, 1)
                    dve.wait_ge(sm_max, c + 1)
                    dve.tensor_tensor(sd[:, :, :], sd[:, :, :], bc(mx[:, :], SEQ), ALU.subtract).then_inc(sm_sub, 1)
                    dve.wait_ge(sm_exp, c + 1)
                    dve.tensor_reduce(rc[:, 0, :], sd[:, :, :], AX_X, ALU.add).then_inc(sm_sum, 1)
                    dve.wait_ge(sm_sum, c + 1)
                    dve.reciprocal(rc[:, 0, :], rc[:, 0, :]).then_inc(sm_rc, 1)
                    dve.wait_ge(sm_rc, c + 1)
                    dve.tensor_scalar(rc[:, 2, :], rc[:, 0, :], odd, None, ALU.mult)
                    dve.tensor_scalar(rc[:, 1, :], rc[:, 0, :], even, None, ALU.mult).then_inc(sm_r01, 1)
                    dve.wait_ge(sm_r01, c + 1)
                    dve.tensor_tensor(p32[:, :, 0:SEQ], sd[:, :, :], bc(rc[:, 1, :], SEQ), ALU.mult).then_inc(p_even, 1)
                    dve.wait_ge(p_even, c + 1)
                    dve.wait_ge(p_odd, c + 1)
                    dve.transpose(pt[:, :, :].rearrange("p n i -> p (n i)"), p32[:, :, :].rearrange("p n j -> p (n j)")).then_inc(pt_done, 1)
                if s in (8, 9):
                    m = s - 8
                    dve.wait_ge(pv_t[m], c + 1)
                    dve.scalar_tensor_tensor(of[:, m, :].rearrange("p (n j) -> p n j", j=Q), pre_blk[:, 0::2, :], even,
                                             tmp[:, :].rearrange("p (n j) -> p n j", j=Q), ALU.mult, ALU.add).then_inc(o_done[m], 1)
                    dve.wait_ge(o_hi[m], c + 1)
                    dve.tensor_tensor(by_group(oht[:, 1, m, :]), grouped(of[:, m, :]), by_group(oht[:, 0, m, :]).bitcast(F32),
                                      ALU.subtract).then_inc(o_lo[m], 1)
                if s == 10:
                    dve.wait_ge(wo_mm, c + 1)
                    dve.wait_ge(h0_bo, c + 1)
                    dve.tensor_tensor(hres[:, :, :], pre_tok, hres[:, :, :], ALU.add).then_inc(h1_done, 1)
                    dve.wait_ge(h1_done, c + 1)
                    norm_stats(1, c)
                if s == 11:
                    norm_apply(1, c)
                if s == 14:
                    routing(c)

            def routing(c):
                done = [ROUTE_OPS * c]

                def step(ins):
                    done[0] = done[0] + 1
                    ins.then_inc(route, 1)
                    dve.wait_ge(route, done[0])

                z = rt[:, 0:2, :].rearrange("p a n -> p (a n)").rearrange("p (t a e) -> p t a e", t=NT, a=2)
                logit = rt[:, 2, :].rearrange("p (t e) -> p t e", t=NT)
                dve.wait_ge(lg_tok, c + 1)
                step(dve.tensor_tensor(logit, z[:, :, 0, :], z[:, :, 1, :], ALU.add))
                dve.wait_ge(lg_exp, c + 1)
                score, sc, masked = rt[:, 3, :], rt[:, 2, :], rt[:, 0, :]
                step(dve.tensor_scalar(score, rt[:, 3, :], 1.0, None, ALU.add))
                step(dve.reciprocal(score, score))
                step(dve.tensor_tensor(sc.rearrange("p (t e) -> p t e", t=NT), score.rearrange("p (t e) -> p t e", t=NT),
                                       row[:, 2 * D:2 * D + NE].unsqueeze(1).to_broadcast([P, NT, NE]), ALU.add))
                pair = sc.rearrange("p (g a b) -> p g a b", a=2, b=2)
                big = rg[:, 0:2, :].rearrange("p a n -> p (a n)").rearrange("p (g a) -> p g a", a=2)
                small = rg[:, 2:4, :].rearrange("p a n -> p (a n)").rearrange("p (g a) -> p g a", a=2)
                dve.tensor_tensor(big, pair[:, :, :, 0], pair[:, :, :, 1], ALU.max)
                step_pair = dve.tensor_tensor(small, pair[:, :, :, 0], pair[:, :, :, 1], ALU.min)
                step(step_pair)
                dve.tensor_tensor(rg[:, 4, :], big[:, :, 0], big[:, :, 1], ALU.max)
                dve.tensor_tensor(rg[:, 5, :], big[:, :, 0], big[:, :, 1], ALU.min)
                step(dve.tensor_tensor(rg[:, 6, :], small[:, :, 0], small[:, :, 1], ALU.max))
                step(dve.tensor_tensor(rg[:, 7, :], rg[:, 5, :], rg[:, 6, :], ALU.max))
                step(dve.tensor_tensor(rg[:, 8, :], rg[:, 4, :], rg[:, 7, :], ALU.add))
                rank(step, rg[:, 8, :], rg[:, 9, :], NGRP, tri_s[:, NE * NE:NE * NE + NGRP * NGRP])
                step(dve.tensor_scalar(rg[:, 9, :], rg[:, 9, :], float(TOPG), None, ALU.is_lt))
                step(dve.tensor_tensor(masked.rearrange("p (g a) -> p g a", a=EPG), sc.rearrange("p (g a) -> p g a", a=EPG),
                                       bc(rg[:, 9, :], EPG), ALU.mult))
                rank(step, masked, rt[:, 1, :], NE, tri_s[:, 0:NE * NE])
                w = rt[:, 2, :]
                step(dve.scalar_tensor_tensor(w, rt[:, 1, :], float(TOPK), score, ALU.is_lt, ALU.mult))
                tot = rg[:, 0, 0:NT]
                step(dve.tensor_reduce(tot, w.rearrange("p (t e) -> p t e", t=NT), AX_X, ALU.add))
                step(dve.tensor_scalar(tot, tot, 1e-20, None, ALU.add))
                step(dve.reciprocal(tot, tot))
                wt = w.rearrange("p (t e) -> p t e", t=NT)
                step(dve.scalar_tensor_tensor(wt, wt, ROUTE_SCALE, bc(tot, NE), ALU.mult, ALU.mult))
                step(dve.tensor_copy(comb_hl[:, :, 0:NE], wt))
                step(dve.tensor_tensor(comb_hl[:, :, NE:2 * NE], wt, comb_hl[:, :, 0:NE].bitcast(F32), ALU.subtract))

            def rank(step, val, out, n, before):
                r = val.shape[1] // n
                v = val.rearrange("p (r e) -> p r e", e=n)
                mine = v.unsqueeze(3).to_broadcast([P, r, n, n])
                other = v.unsqueeze(2).to_broadcast([P, r, n, n])
                gt, ge = (cmp[:, j, 0:r * n * n].rearrange("p (r e f) -> p r e f", e=n, f=n) for j in range(2))
                dve.tensor_tensor(gt, other, mine, ALU.is_gt)
                step(dve.tensor_tensor(ge, other, mine, ALU.is_ge))
                flat = [cmp[:, j, 0:r * n * n].rearrange("p (r f) -> p r f", r=r) for j in range(2)]
                step(dve.tensor_tensor(flat[1], flat[1], before.unsqueeze(1).to_broadcast([P, r, n * n]), ALU.mult))
                step(dve.tensor_tensor(flat[0], flat[0], flat[1], ALU.max))
                step(dve.tensor_reduce(out, cmp[:, 0, 0:r * n * n].rearrange("p (r e) -> p r e", e=n), AX_X, ALU.add))

            def expert(c, u):
                dve.wait_ge(silu, c * NU + u + 1)
                dve.wait_ge(u_mm, c * NU + u + 1)
                if u >= 2:
                    dve.wait_ge(h_lo, c * NU + u - 1)
                if u < NSH:
                    dve.tensor_tensor(h_s[:, u % 2, :], sg[:, :], pu[:, :], ALU.mult).then_inc(gated, 1)
                    dve.wait_ge(gated, c * NU + u + 1)
                    dve.sem_inc(weighted, 1)
                else:
                    dve.tensor_tensor(h_s[:, u % 2, :], sg[:, :], pu[:, :], ALU.mult).then_inc(gated, 1)
                    dve.wait_ge(gated, c * NU + u + 1)
                    dve.wait_ge(w_mm, c * NE + u - NSH + 1)
                    dve.tensor_tensor(h_s[:, u % 2, :], h_s[:, u % 2, :], pw[:, :], ALU.mult).then_inc(weighted, 1)

            def finish(c):
                dve.wait_ge(down, NU * (c + 1))
                dve.tensor_copy(out_s[:, :, :], po[:, :, :]).then_inc(out_sb, 1)
                dve.wait_ge(out_sb, c + 1)
                dve.sem_inc(po_free, 1)

            dve.memset(rstd[:, 3, :], EPS)
            dve.memset(rstd[:, 1, :], -0.5).then_inc(consts, 1)
            dve.sem_inc(po_free, 1)
            dve.memset(rw_h[:, :, :].bitcast(F32), 0.0)
            dve.memset(rw_hl[:, :, :].bitcast(F32), 0.0).then_inc(consts, 1)
            dve.wait_ge(small_in, 64)
            dve.tensor_scalar(bq_s[:, :], col[:, C_BQ:C_BQ + KD], SCALE, None, ALU.mult)
            dve.tensor_scalar(bk_e[:, :], col[:, C_BK:C_BK + KD], even, None, ALU.mult)
            dve.tensor_tensor(pick[:, :], ident_s[0:2 * NE, 0:NE], ident_s[0:2 * NE, NE:2 * NE], ALU.add).then_inc(consts, 1)
            dve.wait_ge(aw_h_done, 1)
            dve.tensor_tensor(aw_l[:, :], aw_s[:, 0:W_R], aw_h[:, :].bitcast(F32), ALU.subtract).then_inc(aw_l_done, 1)
            r = aw_s[:, W_R:W_END].rearrange("p (k e) -> p k e", k=KD)
            dve.wait_ge(consts, 3)
            dve.tensor_copy(rw_h[:, :, 0:NE], r)
            dve.tensor_copy(rw_hl[:, :, 0:NE], r).then_inc(consts, 1)
            dve.wait_ge(consts, 4)
            dve.tensor_tensor(rw_hl[:, :, NE:2 * NE], r, rw_h[:, :, 0:NE].bitcast(F32), ALU.subtract).then_inc(rw_done, 1)
            for s in range(STEPS):
                prefix(s, 0, first=True)
            for u in range(NU):
                expert(0, u)
            finish(0)
            for s in range(STEPS):
                prefix(s, 1)
            with dve.Fori(1, NCH - 1) as c:
                for u in range(NU):
                    expert(c, u)
                finish(c)
                for s in range(STEPS):
                    prefix(s, c + 1)
            for u in range(NU):
                expert(NCH - 1, u)
            finish(NCH - 1)

        @block.gpsimd
        def _(pool):
            def rsqrt(i, c):
                pool.wait_ge(ln_mv[i], c + 1)
                pool.tensor_tensor(rstd[:, 0, :], mv[:, :, 1], rstd[:, 3, :], ALU.add).then_inc(ln_var[i], 1)
                pool.wait_ge(ln_var[i], c + 1)
                pool.tensor_tensor(rstd[:, 2, :], rstd[:, 0, :], rstd[:, 1, :], ALU.pow).then_inc(ln_rs[i], 1)

            def prefix(s, c):
                if s == 0:
                    rsqrt(0, c)
                if s == 1:
                    pool.wait_ge(ln_xn[0], c + 1)
                    pool.tensor_tensor(hres[:, :, :], hres[:, :, :], row[:, D:2 * D].unsqueeze(1).to_broadcast([P, NT, D]), ALU.add)\
                        .then_inc(h0_bo, 1)
                if s == 7:
                    pool.wait_ge(sm_r01, c + 1)
                    pool.tensor_tensor(p32[:, :, SEQ:Q], sd[:, :, :], bc(rc[:, 2, :], SEQ), ALU.mult).then_inc(p_odd, 1)
                if s == 10:
                    rsqrt(1, c)

            def expert(c, u):
                pool.wait_ge(h_hi, c * NU + u + 1)
                if u >= 2:
                    pool.wait_ge(down, c * NU + u - 1)
                pool.tensor_tensor(hl[:, u % 2, :], h_s[:, u % 2, :], hh[:, u % 2, :].bitcast(F32), ALU.subtract).then_inc(h_lo, 1)

            def split_low(u):
                pool.wait_ge(fw_h_done, u + 1)
                pool.tensor_tensor(ffn_l[:, u, :], stage[:, u % 2, :], ffn_h[:, u, :].bitcast(F32), ALU.subtract).then_inc(fw_l_done, 1)

            pool.wait_ge(consts, 1)
            pool.wait_ge(small_in, 64)
            for u in range(4):
                split_low(u)
            for s in range(STEPS):
                prefix(s, 0)
                if s + 4 < NU:
                    split_low(s + 4)
            for u in range(STEPS + 4, NU):
                split_low(u)
            for u in range(NU):
                expert(0, u)
            for s in range(STEPS):
                prefix(s, 1)
            with pool.Fori(1, NCH - 1) as c:
                for u in range(NU):
                    expert(c, u)
                for s in range(STEPS):
                    prefix(s, c + 1)
            for u in range(NU):
                expert(NCH - 1, u)


def kernel(**inputs):
    import numpy as np
    import concourse.bacc as bacc
    from concourse.bass_utils import run_bass_kernel_spmd

    g = {k: np.asarray(v) for k, v in inputs.items()}
    C, F, PER = g["L0_tok_conv_w"].shape
    x = g["x"].reshape(TOK, PER, C).transpose(2, 1, 0).reshape(P, TOK)
    emb = g["L0_tok_emb_w"].T.reshape(C // 2, P, D).transpose(1, 0, 2).reshape(P, -1)
    conv = np.zeros((P, C // 2, 2, PER), np.float32)
    for ch in range(C):
        conv[(ch % 2) * F:(ch % 2) * F + F, ch // 2, ch % 2] = g["L0_tok_conv_w"][ch]
    tok = np.concatenate([emb, conv.reshape(P, -1)], 1)

    def halves(w):
        return w.reshape(KD, P, -1).transpose(1, 0, 2).reshape(P, -1)

    twice = lambda a, axis: np.concatenate([a, a], axis)
    attn = np.concatenate([halves(g["L0_attn_Wq"]), halves(twice(g["L0_attn_Wl"], 1)), twice(g["L0_attn_Wk"], 0),
                           twice(g["L0_attn_Wv"], 0), halves(g["L0_attn_Wo"]), halves(g["L0_ffn_router_weight"].T)], 1)
    experts = []
    for e in range(NSH):
        s = slice(e * P, e * P + P)
        experts.append((g["L0_ffn_sh_gate_w"][s], g["L0_ffn_sh_up_w"][s], g["L0_ffn_sh_down_w"][:, s]))
    for e in range(NE):
        experts.append((g["L0_ffn_gate_w"][e], g["L0_ffn_up_w"][e], g["L0_ffn_down_w"][e]))
    ffn = np.stack([np.concatenate([halves(a.T), halves(b.T), d.T], 1) for a, b, d in experts])
    half = (np.arange(P) // SEQ) % 2
    cols = np.concatenate([g["L0_attn_bq"].reshape(KD, P).T, twice(g["L0_attn_bl"], 0)[:, None], g["L0_attn_bk"].reshape(KD, P).T,
                           g["L0_attn_bv"].reshape(KD, P).T, (half == 0)[:, None], (half == 1)[:, None]], 1)
    rows = np.concatenate([g["L0_tok_emb_b"], g["L0_attn_bo"], g["L0_ffn_e_bias"]])
    tri = np.concatenate([np.tril(np.ones((n, n)), -1).ravel() for n in (NE, NGRP)])
    arrays = {"x_t": x, "tok_w": tok, "attn_w": attn, "ffn_w": ffn, "cols": cols, "rows": np.broadcast_to(rows, (P, rows.size)),
              "tri": np.broadcast_to(tri, (P, tri.size)), "ident": np.eye(P)}
    arrays = {k: np.ascontiguousarray(a, dtype=np.float32) for k, a in arrays.items()}

    nc = bacc.Bacc("TRN2", target_bir_lowering=False, num_devices=1)
    args = [nc.dram_tensor(n, a.shape, F32, kind="ExternalInput").ap() for n, a in arrays.items()]
    out = nc.dram_tensor("out_t", (D, TOK), F32, kind="ExternalOutput").ap()
    tower(nc, *args, out.rearrange("(k p) n -> p k n", p=P))
    r = run_bass_kernel_spmd(nc, [arrays], core_ids=[0])
    return np.ascontiguousarray(r.results[0]["out_t"].T).reshape(TOK // SEQ, SEQ, D)
```

```python
from contextlib import ExitStack

import concourse.bass as bass
from concourse import mybir

F32 = mybir.dt.float32
F32R = mybir.dt.float32r
ALU = mybir.AluOpType
ACT = mybir.ActivationFunctionType
AX_X = mybir.AxisListType.X

P = 128
TOK = 2048
SEQ = 16
D = 256
KD = D // P
CH = 512
NCH = TOK // CH
NT = CH // P
Q = 32
NQ = P // Q
NB = 2 * NQ * NT * 2
NE = 16
NSH = 2
NU = NE + NSH
NBUF = 3
LAG = 2
NGRP, TOPG, TOPK = 4, 2, 4
EPG = NE // NGRP
SCALE = 16 ** -0.5
ROUTE_SCALE = 2.5
EPS = 1e-5

C_BQ, C_BL, C_BK, C_BV, C_EVEN, C_ODD, NCOL = 0, 2, 3, 5, 7, 8, 9
W_Q, W_L, W_K, W_V, W_O, W_R, W_END = 0, 512, 768, 1024, 1280, 1792, 1824
STEPS = 25
ROUTE_OPS = 25
ROUTE_AT = (0, 1, 14, 15, 17)

OWN = {22: 0, 23: 1, 24: 2}
NEXT = {0: 3, 1: 4, 2: 6, 3: 8, 4: 9, 5: 10, 6: 12, 7: 13, 8: 15, 9: 17, 10: 18, 11: 20, 12: 21, 13: 23, 14: 25,
        15: 27, 16: 29, 17: 30, 18: 31, 19: 32, 20: 33, 21: 34}


def gap_steps(u, side, own, following):
    g = 2 * u + side
    return [(n, own) for n, at in OWN.items() if at == g and own is not None] + \
           [(n, following) for n, at in NEXT.items() if at == g and following is not None]


def tower(nc, x_t, tok_w, attn_w, ffn_w, cols, rows, tri, ident, out_t):
    at = {"end": (nc.sbuf_base + 63) // 64 * 64}

    def sb(name, shape, dt=F32, over=None):
        size = 4
        for n in shape[1:]:
            size *= n
        start = at[over] if over else at["end"]
        at[name] = start
        if not over:
            at["end"] += (size + 31) // 32 * 32
        assert start + size <= nc.sbuf_usable_end, (name, start, size)
        return nc.alloc_sbuf_tensor_at(name, shape, dt, offset=start)

    with ExitStack() as ctx:
        def sem(name):
            return ctx.enter_context(nc.semaphore(name))

        def pair(name):
            return sem(name + "0"), sem(name + "1")

        def psum(name, shape):
            return ctx.enter_context(nc.psum_tensor(name, shape, F32))

        ffn_h = sb("ffn_h", [P, NU, 3 * D], F32R)
        ffn_l = sb("ffn_l", [P, NU, 3 * D], F32R)
        aw_h = sb("aw_h", [P, W_R], F32R)
        aw_l = sb("aw_l", [P, W_R], F32R)
        rw_hl = sb("rw_hl", [P, KD, P], F32R)
        w_tok = sb("w_tok", [P, D])
        ident_s = sb("ident_s", [P, P])
        pick = sb("pick", [2 * NE, NE], F32R)
        col = sb("col", [P, NCOL])
        bq_s = sb("bq_s", [P, KD])
        bk_e = sb("bk_e", [P, KD])
        row = sb("row", [P, 2 * D + NE])
        tri_s = sb("tri_s", [P, NE * NE + NGRP * NGRP])
        even, odd = col[:, C_EVEN:C_EVEN + 1], col[:, C_ODD:C_ODD + 1]

        x_s = sb("x_s", [P, CH])
        hres = sb("hres", [P, NT, D])
        q_t = sb("q_t", [P, KD, CH])
        out_s = sb("out_s", [P, KD, CH], over="q_t")
        s1 = sb("s1", [P, CH], F32R)
        v_s = sb("v_s", [P, NT, D])
        xn = sb("xn", [P, NT, D])
        sd = sb("sd", [P, NB, SEQ], over="xn")
        of = sb("of", [P, KD, CH], over="xn")
        keo = sb("keo", [P, KD, 2, CH])
        pt = sb("pt", [P, NB, Q], over="keo")
        cmp = sb("cmp", [P, 2, NT * NE * NE], over="keo")
        emb_s = sb("emb_s", [P, 4 * (D + Q)], over="keo")
        xnt = sb("xnt", [P, 2, KD, CH], F32R)
        oht = sb("oht", [P, 2, KD, CH], F32R, over="xnt")
        p32 = sb("p32", [P, NB, Q], over="xnt")
        tmp = sb("tmp", [P, CH])
        xn2 = sb("xn2", [P, 2, 2, KD, CH], F32R)
        comb_t = sb("comb_t", [2 * NE, CH], F32R)
        comb_hl = sb("comb_hl", [P, NT, 2 * NE], F32R)
        bn = sb("bn", [P, NT, 6])
        mv = sb("mv", [P, NT, 2])
        rstd = sb("rstd", [P, 4, NT])
        mx = sb("mx", [P, NB])
        rc = sb("rc", [P, 3, NB])
        rt = sb("rt", [P, 4, NT * NE])
        rg = sb("rg", [P, 10, NT * NGRP])
        sg = sb("sg", [P, CH])
        h_s = sb("h_s", [P, NBUF, CH])
        hh = sb("hh", [P, NBUF, CH], F32R)
        hl = sb("hl", [P, NBUF, CH], F32R)
        aw_s = sb("aw_s", [P, W_END], over="h_s")
        at["stage"] = at["xn2"] + 2 * KD * CH * 4
        stage = sb("stage", [P, 2, 3 * D], over="stage")

        pre = psum("pre", [P, 2, 512])
        pg = psum("pg", [P, 512])
        pu = psum("pu", [P, 2, 512])
        pw = psum("pw", [P, 512])
        po = psum("po", [P, KD, 512])
        pre_tok = pre[:, :, :].rearrange("p b (t d) -> p (b t) d", d=D)
        pre_blk = pre[:, :, :].rearrange("p b (n j) -> p (b n) j", j=Q)

        tok_in, small_in, aw_in, x_in = sem("tok_in"), sem("small_in"), sem("aw_in"), sem("x_in")
        ffn_in = [sem("ffn_in0"), sem("ffn_in1")]
        consts, wtok_mm, wtok_done = sem("consts"), sem("wtok_mm"), sem("wtok_done")
        aw_h_done, aw_l_done, rw_done = sem("aw_h_done"), sem("aw_l_done"), sem("rw_done")
        fw_h_done, fw_l_done = sem("fw_h_done"), sem("fw_l_done")
        h0_mm, h0_sum, h0_done, h0_bo = sem("h0_mm"), sem("h0_sum"), sem("h0_done"), sem("h0_bo")
        ln_bn, ln_mv, ln_var, ln_rs, ln_xn = (pair(x) for x in ("ln_bn", "ln_mv", "ln_var", "ln_rs", "ln_xn"))
        xn_tr, xn_hi, xn_lo = pair("xn_tr"), pair("xn_hi"), pair("xn_lo")
        q_mm, q_done = pair("q_mm"), pair("q_done")
        lat_mm, lat_f, lat_h, lat_l = (sem(x) for x in ("lat_mm", "lat_f", "lat_h", "lat_l"))
        v_mm, v_done = sem("v_mm"), sem("v_done")
        k_mm, k_even, k_odd = pair("k_mm"), pair("k_even"), pair("k_odd")
        sc_mm, sc_t, sc_done = pair("sc_mm"), pair("sc_t"), pair("sc_done")
        sc_row, pv_row = (pair("sc_row0"), pair("sc_row1")), (pair("pv_row0"), pair("pv_row1"))
        sm_max, sm_sub, sm_exp, sm_sum, sm_rc, sm_r01 = (sem(x) for x in ("sm_max", "sm_sub", "sm_exp", "sm_sum", "sm_rc", "sm_r01"))
        p_even, p_odd, pt_done = sem("p_even"), sem("p_odd"), sem("pt_done")
        pv_mm, pv_t, o_done, o_hi, o_lo = (pair(x) for x in ("pv_mm", "pv_t", "o_done", "o_hi", "o_lo"))
        wo_mm, h1_done = sem("wo_mm"), sem("h1_done")
        lg_mm, lg_sb, lg_tr, lg_tok, lg_exp = (sem(x) for x in ("lg_mm", "lg_sb", "lg_tr", "lg_tok", "lg_exp"))
        route = sem("route")
        comb_tr, comb_done = sem("comb_tr"), sem("comb_done")
        res_mm = sem("res_mm")
        g_mm, u_mm = sem("g_mm"), sem("u_mm")
        silu, gated, weighted, h_hi, h_lo = sem("silu"), sem("gated"), sem("weighted"), sem("h_hi"), sem("h_lo")
        w_mm, down = sem("w_mm"), sem("down")
        po_free = sem("po_free")
        out_sb, stored = sem("out_sb"), sem("stored")

        block = ctx.enter_context(nc.Block())

        def par(c):
            return c % 2

        def bc(ap, n):
            return ap.unsqueeze(len(ap.shape)).to_broadcast([*ap.shape, n])

        def value(eng, n):
            return n if isinstance(n, int) else eng.snap(n)

        def grouped(ap):
            return ap.rearrange("p (b t n) -> p b t n", b=NQ, t=NT)

        def by_group(ap):
            return ap.rearrange("p (t b n) -> p b t n", b=NQ, t=NT)

        @block.sync
        def _(sp):
            def load_expert(u):
                if u >= 2:
                    sp.wait_ge(fw_h_done, u - 1)
                    sp.wait_ge(fw_l_done, u - 1)
                sp.dma_start(stage[:, u % 2, :], ffn_w[u]).then_inc(ffn_in[u % 2], 16)

            def load_x(c):
                sp.wait_ge(h0_mm, c)
                sp.dma_start(x_s[:, :], x_t[:, bass.ds(c * CH, CH)]).then_inc(x_in, 16)

            def store(c):
                sp.wait_ge(out_sb, c + 1)
                sp.dma_start(out_t[:, :, bass.ds(c * CH, CH)], out_s[:, :, :]).then_inc(stored, 16)

            sp.dma_start(emb_s[:, :], tok_w).then_inc(tok_in, 16)
            sp.dma_start(x_s[:, :], x_t[:, 0:CH]).then_inc(x_in, 16)
            sp.dma_start(col[:, :], cols).then_inc(small_in, 16)
            sp.dma_start(row[:, :], rows).then_inc(small_in, 16)
            sp.dma_start(ident_s[:, :], ident).then_inc(small_in, 16)
            sp.dma_start(tri_s[:, :], tri).then_inc(small_in, 16)
            sp.dma_start(aw_s[:, :], attn_w).then_inc(aw_in, 16)
            load_x(1)
            for u in range(NU):
                load_expert(u)
            with sp.Fori(0, NCH - 2) as c:
                load_x(c + 2)
                store(c)
            store(NCH - 2)
            store(NCH - 1)
            sp.wait_ge(stored, 16 * NCH)

        @block.tensor
        def _(pe):
            def split_mm(out, w_at, x_at):
                i, n = 0, 3 * KD
                for k in range(KD):
                    for a, b in ((0, 0), (0, 1), (1, 0)):
                        last = pe.matmul(out, w_at(a, k), x_at(b, k), start=i == 0, stop=i == n - 1)
                        i += 1
                return last

            def transpose_xn(i):
                for k in range(KD):
                    for t in range(NT):
                        last = pe.transpose(pre[:, k, t * P:(t + 1) * P], xn[:, t, k * P:(k + 1) * P], ident_s[:, :])
                last.then_inc(xn_tr[i], 1)

            def project(bank, w0, stride):
                return split_mm(pre[:, bank, :], lambda a, k: (aw_h, aw_l)[a][:, w0 + k * stride:w0 + k * stride + P],
                                lambda b, k: xnt[:, b, k, :])

            def k_half(m, bank):
                for i, w in enumerate((aw_h, aw_l)):
                    last = pe.matmul(pre[:, bank, :], w[:, W_K + m * P:W_K + m * P + P], s1[:, :], start=i == 0, stop=i == 1)
                last.then_inc(k_mm[m], 1)

            def prefix(s, c, first=False):
                if s == 0:
                    pe.wait_ge(x_in, 16 * c + 16)
                    if not first:
                        pe.wait_ge(comb_done, c)
                    for t in range(NT):
                        last = pe.matmul(pre_tok[:, t, :], x_s[:, t * P:(t + 1) * P], w_tok[:, :], start=True, stop=True)
                    last.then_inc(h0_mm, 1)
                if s == 3:
                    pe.wait_ge(ln_xn[0], c + 1)
                    transpose_xn(0)
                if s == 4:
                    pe.wait_ge(xn_hi[0], c + 1)
                    pe.wait_ge(xn_lo[0], c + 1)
                    project(0, W_L, P).then_inc(lat_mm, 1)
                    project(1, W_Q, D).then_inc(q_mm[0], 1)
                if s == 5:
                    pe.wait_ge(lat_f, c + 1)
                    project(0, W_Q + P, D).then_inc(q_mm[1], 1)
                    pe.wait_ge(lat_l, c + 1)
                    pe.wait_ge(q_done[0], c + 1)
                    k_half(0, 1)
                if s == 6:
                    pe.wait_ge(q_done[1], c + 1)
                    k_half(1, 0)
                if s == 7:
                    for m in range(KD):
                        pe.wait_ge(k_even[m], c + 1)
                    for t in range(NT):
                        for i, w in enumerate((aw_h, aw_l)):
                            last = pe.matmul(pre_tok[:, t, :], s1[:, t * P:(t + 1) * P], w[:, W_V:W_V + D], start=i == 0, stop=i == 1)
                    last.then_inc(v_mm, 1)
                if s in (8, 9):
                    m = s - 8
                    n = value(pe, c + 1)
                    pe.wait_ge(tok_in, 16)
                    pe.wait_ge(v_done if m == 0 else sc_done[0], n)
                    out = pre[:, :, :].rearrange("p b (g t n) -> p (b g) t n", g=2, t=NT)
                    for g in (0, 2, 1, 3):
                        if g % 2:
                            pe.wait_ge(tok_in, 16)
                            pe.wait_ge(sc_row[m][g // 2], n)
                        rows_g = slice(g * Q, g * Q + Q)
                        for t in range(NT):
                            for b in range(NQ):
                                tok = slice(t * P + b * Q, t * P + b * Q + Q)
                                last = pe.matmul(out[b * Q:b * Q + Q, g, t, :], q_t[rows_g, m, tok], keo[rows_g, m, :, tok],
                                                 start=True, stop=True, tile_position=(g * Q, b * Q))
                        if g % 2 == 0:
                            last.then_inc(sc_row[m][g // 2], 1)
                    last.then_inc(sc_mm[m], 1)
                if s in (13, 14):
                    m = s - 13
                    n = value(pe, c + 1)
                    pe.wait_ge(tok_in, 16)
                    pe.wait_ge(pt_done if m == 0 else o_done[0], n)
                    out = pre[:, :, :].rearrange("p b (g t n) -> p (b g) t n", g=2, t=NT)
                    for b in (0, 2, 1, 3):
                        if b % 2:
                            pe.wait_ge(tok_in, 16)
                            pe.wait_ge(pv_row[m][b // 2], n)
                        rows_b = slice(b * Q, b * Q + Q)
                        for t in range(NT):
                            for g in range(NQ):
                                blk = ((m * NQ + g) * NT + t) * 2
                                last = pe.matmul(out[g * Q:g * Q + Q, b, t, :], v_s[rows_b, t, m * P + g * Q:m * P + g * Q + Q],
                                                 pt[rows_b, blk:blk + 2, :], start=True, stop=True, tile_position=(b * Q, g * Q))
                        if b % 2 == 0:
                            last.then_inc(pv_row[m][b // 2], 1)
                    last.then_inc(pv_mm[m], 1)
                if s == 15:
                    for m in range(KD):
                        pe.wait_ge(o_hi[m], c + 1)
                        pe.wait_ge(o_lo[m], c + 1)
                    for t in range(NT):
                        last = split_mm(pre_tok[:, t, :], lambda a, m: oht[:, a, m, t * P:(t + 1) * P],
                                        lambda b, m: (aw_h, aw_l)[b][:, W_O + m * D:W_O + m * D + D])
                    last.then_inc(wo_mm, 1)
                if s == 17:
                    pe.wait_ge(ln_xn[1], c + 1)
                    transpose_xn(1)
                if s == 18:
                    pe.wait_ge(xn_hi[1], c + 1)
                    pe.wait_ge(xn_lo[1], c + 1)
                    if first:
                        pe.wait_ge(rw_done, 1)
                    for i in range(2 * KD):
                        last = pe.matmul(pre[:, 0, :], rw_hl[:, i % KD, :], xn2[:, par(c), i // KD, i % KD, :],
                                         start=i == 0, stop=i == 2 * KD - 1)
                    last.then_inc(lg_mm, 1)
                if s == 19:
                    n = value(pe, c + 1)
                    pe.wait_ge(tok_in, 16)
                    pe.wait_ge(lg_sb, n)
                    for t in range(NT):
                        last = pe.transpose(pre[:, 1, t * 2 * NE:(t + 1) * 2 * NE], tmp[0:2 * NE, t * P:(t + 1) * P],
                                            ident_s[0:2 * NE, 0:2 * NE])
                    last.then_inc(lg_tr, 1)
                if s == 24:
                    n = value(pe, ROUTE_OPS * (c + 1))
                    pe.wait_ge(tok_in, 16)
                    pe.wait_ge(route, n)
                    for t in range(NT):
                        last = pe.transpose(pre[0:2 * NE, 0, t * P:(t + 1) * P], comb_hl[:, t, :].bitcast(F32), ident_s[:, :])
                    last.then_inc(comb_tr, 1)

            def residual(c):
                pe.wait_ge(po_free, c + 1)
                pe.wait_ge(h1_done, c + 1)
                for k in range(KD):
                    for t in range(NT):
                        last = pe.matmul(po[:, k, t * P:(t + 1) * P], hres[:, t, k * P:(k + 1) * P], ident_s[:, :],
                                         is_transpose=True, start=t == 0, stop=False, skip_group_check=True)
                last.then_inc(res_mm, 1)

            def ffn_mm(c, u, out, off):
                return split_mm(out, lambda a, k: (ffn_h, ffn_l)[a][:, u, off + k * P:off + k * P + P],
                                lambda b, k: xn2[:, par(c), b, k, :])

            def expert(c, u, own, following, first=False):
                if first:
                    pe.wait_ge(fw_l_done, u + 1)
                if u > 0:
                    pe.wait_ge(silu, c * NU + u)
                ffn_mm(c, u, pg[:, :], 0).then_inc(g_mm, 1)
                for n, cn in gap_steps(u, 0, own, following):
                    prefix(n, cn)
                if u > 1:
                    pe.wait_ge(gated, c * NU + u - 1)
                ffn_mm(c, u, pu[:, u % 2, :], D).then_inc(u_mm, 1)
                if u >= NSH:
                    e = u - NSH
                    n = value(pe, c + 1 if e == 0 else c * NU + u)
                    pe.wait_ge(small_in, 64)
                    pe.wait_ge(comb_done if e == 0 else weighted, n)
                    pe.matmul(pw[:, :], pick[:, e:e + 1].to_broadcast([2 * NE, P]), comb_t[:, :],
                              start=True, stop=True).then_inc(w_mm, 1)
                if u >= LAG:
                    down_mm(c, u - LAG)
                for n, cn in gap_steps(u, 1, own, following):
                    prefix(n, cn)

            def down_mm(c, u):
                pe.wait_ge(h_lo, c * NU + u + 1)
                for k in range(KD):
                    for i, (w, x) in enumerate(((ffn_h, hh), (ffn_h, hl), (ffn_l, hh))):
                        last = pe.matmul(po[:, k, :], w[:, u, 2 * D + k * P:2 * D + k * P + P], x[:, u % NBUF, :],
                                         start=False, stop=u == NU - 1 and i == 2, skip_group_check=True)
                last.then_inc(down, 1)

            def chunk(c, own, following, first=False):
                residual(c)
                for u in range(NU):
                    expert(c, u, own, following, first)
                for u in range(NU - LAG, NU):
                    down_mm(c, u)

            pe.wait_ge(tok_in, 16)
            for i in range(4):
                last = pe.matmul(pre[i * Q:i * Q + Q, 0, 0:D], emb_s[:, 4 * D + i * Q:4 * D + i * Q + Q], emb_s[:, i * D:i * D + D],
                                 start=True, stop=True)
            last.then_inc(wtok_mm, 1)
            pe.wait_ge(wtok_done, 1)
            pe.wait_ge(small_in, 64)
            for s in range(STEPS):
                if s == 4:
                    pe.wait_ge(aw_h_done, 1)
                    pe.wait_ge(aw_l_done, 1)
                prefix(s, 0, first=True)
            chunk(0, None, 1, first=True)
            with pe.Fori(1, NCH - 1) as c:
                chunk(c, c, c + 1)
            chunk(NCH - 1, NCH - 1, None)

        @block.scalar
        def _(act):
            def prefix(s, c, first=False, early=False):
                if s in (3, 17):
                    i = int(s == 17)
                    act.wait_ge(xn_tr[i], c + 1)
                    if early and i == 1:
                        act.wait_ge(fw_l_done, NU)
                    dst = xnt[:, 0, :, :] if i == 0 else xn2[:, par(c), 0, :, :]
                    act.activation(dst, pre[:, :, :], ACT.Copy).then_inc(xn_hi[i], 1)
                if s == 4:
                    act.wait_ge(lat_f, c + 1)
                    act.activation(s1[:, :], tmp[:, :], ACT.Copy).then_inc(lat_h, 1)
                    if not (first or early):
                        act.wait_ge(stored, 16 * (c - 1))
                if s in (4, 5):
                    m = s - 4
                    act.wait_ge(q_mm[m], c + 1)
                    act.activation(q_t[:, m, :], pre[:, 1 - m, :], ACT.Identity, bias=bq_s[:, m:m + 1], scale=SCALE).then_inc(q_done[m], 1)
                if s in (5, 6):
                    m = s - 5
                    act.wait_ge(k_odd[m], c + 1)
                    act.activation(keo[:, m, 0, :], pre[:, 1 - m, :], ACT.Identity, bias=bk_e[:, m:m + 1], scale=even).then_inc(k_even[m], 1)
                if s == 7:
                    act.wait_ge(v_mm, c + 1)
                    act.activation(v_s[:, :, :], pre_tok, ACT.Copy).then_inc(v_done, 1)
                if s in (8, 9):
                    m = s - 8
                    act.wait_ge(sc_mm[m], c + 1)
                    if m == 1:
                        act.wait_ge(sc_done[0], c + 1)
                    act.activation(tmp[:, :].rearrange("p (n j) -> p n j", j=SEQ), pre_blk[:, :, 0:SEQ], ACT.Identity, bias=0.0, scale=even)\
                       .then_inc(sc_t[m], 1)
                if s == 10:
                    act.wait_ge(sm_sub, c + 1)
                    act.activation(sd[:, :, :], sd[:, :, :], ACT.Exp).then_inc(sm_exp, 1)
                if s in (13, 14):
                    m = s - 13
                    act.wait_ge(pv_mm[m], c + 1)
                    if m == 1:
                        act.wait_ge(o_lo[0], c + 1)
                    act.activation(tmp[:, :].rearrange("p (n j) -> p n j", j=Q), pre_blk[:, 1::2, :], ACT.Identity,
                                   bias=col[:, C_BV + m:C_BV + m + 1], scale=odd).then_inc(pv_t[m], 1)
                    act.wait_ge(o_done[m], c + 1)
                    act.activation(by_group(oht[:, 0, m, :]), grouped(of[:, m, :]), ACT.Copy).then_inc(o_hi[m], 1)
                if s == 18:
                    act.wait_ge(lg_mm, c + 1)
                    act.activation(tmp[0:2 * NE, :], pre[0:2 * NE, 0, :], ACT.Copy).then_inc(lg_sb, 1)
                if s == 19:
                    act.wait_ge(lg_tr, c + 1)
                    act.activation(rt[:, 0:2, :].rearrange("p a n -> p (a n)"), pre[:, 1, 0:NT * 2 * NE], ACT.Copy).then_inc(lg_tok, 1)
                    act.wait_ge(route, ROUTE_OPS * c + 1)
                    act.activation(rt[:, 3, :], rt[:, 2, :], ACT.Exp, scale=-1.0).then_inc(lg_exp, 1)
                if s == 24:
                    act.wait_ge(comb_tr, c + 1)
                    act.activation(comb_t[:, :], pre[0:2 * NE, 0, :], ACT.Copy).then_inc(comb_done, 1)

            def expert(c, u, own, following, early=False):
                act.wait_ge(g_mm, c * NU + u + 1)
                if u > 0:
                    act.wait_ge(gated, c * NU + u)
                act.activation(sg[:, :], pg[:, :], ACT.Silu).then_inc(silu, 1)
                for n, cn in gap_steps(u, 0, own, following):
                    prefix(n, cn, early=early)
                act.wait_ge(weighted, c * NU + u + 1)
                if u >= NBUF:
                    act.wait_ge(down, c * NU + u - NBUF + 1)
                act.activation(hh[:, u % NBUF, :], h_s[:, u % NBUF, :], ACT.Copy).then_inc(h_hi, 1)
                for n, cn in gap_steps(u, 1, own, following):
                    prefix(n, cn, early=early)

            def split_high(u):
                act.wait_ge(ffn_in[u % 2], 16 * (u // 2 + 1))
                act.activation(ffn_h[:, u, :], stage[:, u % 2, :], ACT.Copy).then_inc(fw_h_done, 1)

            act.wait_ge(wtok_mm, 1)
            act.activation(w_tok[:, :], pre[:, 0, 0:D], ACT.Copy).then_inc(wtok_done, 1)
            act.wait_ge(aw_in, 16)
            act.activation(aw_h[:, :], aw_s[:, 0:W_R], ACT.Copy).then_inc(aw_h_done, 1)
            for s in range(STEPS):
                prefix(s, 0, first=True)
                if 3 <= s < 3 + NU:
                    split_high(s - 3)
            for u in range(NU):
                expert(0, u, None, 1, early=True)
            with act.Fori(1, NCH - 1) as c:
                for u in range(NU):
                    expert(c, u, c, c + 1)
            for u in range(NU):
                expert(NCH - 1, u, NCH - 1, None)

        @block.vector
        def _(dve):
            def norm_stats(i, c):
                for t in range(NT):
                    last = dve.bn_stats(bn[:, t, :], hres[:, t, :])
                last.then_inc(ln_bn[i], 1)
                n = value(dve, c + 1)
                dve.wait_ge(small_in, 64)
                dve.wait_ge(ln_bn[i], n)
                for t in range(NT):
                    last = dve.bn_aggr(mv[:, t, :], bn[:, t, :])
                last.then_inc(ln_mv[i], 1)

            def norm_apply(i, c):
                dve.wait_ge(ln_rs[i], c + 1)
                for t in range(NT):
                    last = dve.tensor_scalar(xn[:, t, :], hres[:, t, :], mv[:, t, 0:1], rstd[:, 2, t:t + 1], ALU.subtract, ALU.mult)
                last.then_inc(ln_xn[i], 1)

            def prefix(s, c, first=False):
                if s == 0:
                    dve.wait_ge(h0_mm, c + 1)
                    if not first:
                        dve.wait_ge(res_mm, c)
                    dve.tensor_tensor(hres[:, :, :], pre_tok, row[:, 0:D].unsqueeze(1).to_broadcast([P, NT, D]), ALU.add).then_inc(h0_sum, 1)
                    dve.wait_ge(h0_sum, c + 1)
                    dve.tensor_scalar(hres[:, :, :], hres[:, :, :], 0.0, None, ALU.max).then_inc(h0_done, 1)
                if s == 1:
                    dve.wait_ge(h0_done, c + 1)
                    norm_stats(0, c)
                if s == 2:
                    norm_apply(0, c)
                if s in (3, 17):
                    i = int(s == 17)
                    dve.wait_ge(xn_hi[i], c + 1)
                    hi, lo = (xnt[:, j, :, :] if i == 0 else xn2[:, par(c), j, :, :] for j in range(2))
                    dve.tensor_tensor(lo, pre[:, :, :], hi.bitcast(F32), ALU.subtract).then_inc(xn_lo[i], 1)
                if s == 4:
                    dve.wait_ge(lat_mm, c + 1)
                    dve.tensor_scalar(tmp[:, :], pre[:, 0, :], col[:, C_BL:C_BL + 1], None, ALU.add).then_inc(lat_f, 1)
                    dve.wait_ge(lat_h, c + 1)
                    dve.tensor_tensor(s1[64:128, :], tmp[64:128, :], s1[64:128, :].bitcast(F32), ALU.subtract).then_inc(lat_l, 1)
                if s in (5, 6):
                    m = s - 5
                    dve.wait_ge(k_mm[m], c + 1)
                    dve.tensor_scalar(keo[:, m, 1, :], pre[:, 1 - m, :], col[:, C_BK + m:C_BK + m + 1], odd, ALU.add, ALU.mult).then_inc(k_odd[m], 1)
                if s in (8, 9):
                    m = s - 8
                    dve.wait_ge(sc_t[m], c + 1)
                    dve.scalar_tensor_tensor(sd[:, m * 32:m * 32 + 32, :], pre_blk[:, :, SEQ:Q], odd,
                                             tmp[:, :].rearrange("p (n j) -> p n j", j=SEQ), ALU.mult, ALU.add).then_inc(sc_done[m], 1)
                if s == 10:
                    dve.wait_ge(sc_done[1], c + 1)
                    dve.tensor_reduce(mx[:, :], sd[:, :, :], AX_X, ALU.max).then_inc(sm_max, 1)
                    dve.wait_ge(sm_max, c + 1)
                    dve.tensor_tensor(sd[:, :, :], sd[:, :, :], bc(mx[:, :], SEQ), ALU.subtract).then_inc(sm_sub, 1)
                if s == 11:
                    dve.wait_ge(sm_exp, c + 1)
                    dve.tensor_reduce(rc[:, 0, :], sd[:, :, :], AX_X, ALU.add).then_inc(sm_sum, 1)
                    dve.wait_ge(sm_sum, c + 1)
                    dve.reciprocal(rc[:, 0, :], rc[:, 0, :]).then_inc(sm_rc, 1)
                    dve.wait_ge(sm_rc, c + 1)
                    dve.tensor_scalar(rc[:, 2, :], rc[:, 0, :], odd, None, ALU.mult)
                    dve.tensor_scalar(rc[:, 1, :], rc[:, 0, :], even, None, ALU.mult).then_inc(sm_r01, 1)
                    dve.wait_ge(sm_r01, c + 1)
                    dve.tensor_tensor(p32[:, :, 0:SEQ], sd[:, :, :], bc(rc[:, 1, :], SEQ), ALU.mult).then_inc(p_even, 1)
                if s == 12:
                    dve.wait_ge(p_even, c + 1)
                    dve.wait_ge(p_odd, c + 1)
                    dve.transpose(pt[:, :, :].rearrange("p n i -> p (n i)"), p32[:, :, :].rearrange("p n j -> p (n j)")).then_inc(pt_done, 1)
                if s in (13, 14):
                    m = s - 13
                    dve.wait_ge(pv_t[m], c + 1)
                    dve.scalar_tensor_tensor(of[:, m, :].rearrange("p (n j) -> p n j", j=Q), pre_blk[:, 0::2, :], even,
                                             tmp[:, :].rearrange("p (n j) -> p n j", j=Q), ALU.mult, ALU.add).then_inc(o_done[m], 1)
                    dve.wait_ge(o_hi[m], c + 1)
                    dve.tensor_tensor(by_group(oht[:, 1, m, :]), grouped(of[:, m, :]), by_group(oht[:, 0, m, :]).bitcast(F32),
                                      ALU.subtract).then_inc(o_lo[m], 1)
                if s == 15:
                    dve.wait_ge(wo_mm, c + 1)
                    dve.wait_ge(h0_bo, c + 1)
                    dve.tensor_tensor(hres[:, :, :], pre_tok, hres[:, :, :], ALU.add).then_inc(h1_done, 1)
                    dve.wait_ge(h1_done, c + 1)
                    norm_stats(1, c)
                if s == 16:
                    norm_apply(1, c)
                if s in (19, 20, 21, 22, 23):
                    routing(s, c)

            def routing(s, c):
                done = [ROUTE_OPS * c + ROUTE_AT[s - 19]]

                def step(ins):
                    done[0] = done[0] + 1
                    ins.then_inc(route, 1)
                    dve.wait_ge(route, done[0])

                score, sc, masked, w = rt[:, 3, :], rt[:, 2, :], rt[:, 0, :], rt[:, 2, :]

                def by_tile(ap):
                    return ap.rearrange("p (t e) -> p t e", t=NT)

                if s == 19:
                    z = rt[:, 0:2, :].rearrange("p a n -> p (a n)").rearrange("p (t a e) -> p t a e", t=NT, a=2)
                    dve.wait_ge(lg_tok, c + 1)
                    step(dve.tensor_tensor(by_tile(sc), z[:, :, 0, :], z[:, :, 1, :], ALU.add))
                if s == 20:
                    dve.wait_ge(lg_exp, c + 1)
                    step(dve.tensor_scalar(score, score, 1.0, None, ALU.add))
                    step(dve.reciprocal(score, score))
                    step(dve.tensor_tensor(by_tile(sc), by_tile(score), row[:, 2 * D:2 * D + NE].unsqueeze(1).to_broadcast([P, NT, NE]), ALU.add))
                    pairs = sc.rearrange("p (g a b) -> p g a b", a=2, b=2)
                    big, small = (rg[:, j:j + 2, :].rearrange("p a n -> p (a n)").rearrange("p (g a) -> p g a", a=2) for j in (0, 2))
                    dve.tensor_tensor(big, pairs[:, :, :, 0], pairs[:, :, :, 1], ALU.max)
                    step(dve.tensor_tensor(small, pairs[:, :, :, 0], pairs[:, :, :, 1], ALU.min))
                    dve.tensor_tensor(rg[:, 4, :], big[:, :, 0], big[:, :, 1], ALU.max)
                    dve.tensor_tensor(rg[:, 5, :], big[:, :, 0], big[:, :, 1], ALU.min)
                    step(dve.tensor_tensor(rg[:, 6, :], small[:, :, 0], small[:, :, 1], ALU.max))
                    step(dve.tensor_tensor(rg[:, 7, :], rg[:, 5, :], rg[:, 6, :], ALU.max))
                    step(dve.tensor_tensor(rg[:, 8, :], rg[:, 4, :], rg[:, 7, :], ALU.add))
                    groups = (step, rg[:, 8, :], rg[:, 9, :], NGRP, tri_s[:, NE * NE:NE * NE + NGRP * NGRP])
                    compare(*groups)
                    combine(*groups)
                    count(*groups)
                    step(dve.tensor_scalar(rg[:, 9, :], rg[:, 9, :], float(TOPG), None, ALU.is_lt))
                    step(dve.tensor_tensor(masked.rearrange("p (g a) -> p g a", a=EPG), sc.rearrange("p (g a) -> p g a", a=EPG),
                                           bc(rg[:, 9, :], EPG), ALU.mult))
                experts = (step, masked, rt[:, 1, :], NE, tri_s[:, 0:NE * NE])
                if s == 21:
                    compare(*experts)
                if s == 22:
                    combine(*experts)
                if s == 23:
                    count(*experts)
                if s == 23:
                    step(dve.scalar_tensor_tensor(w, rt[:, 1, :], float(TOPK), score, ALU.is_lt, ALU.mult))
                    tot = rg[:, 0, 0:NT]
                    step(dve.tensor_reduce(tot, by_tile(w), AX_X, ALU.add))
                    step(dve.tensor_scalar(tot, tot, 1e-20, None, ALU.add))
                    step(dve.reciprocal(tot, tot))
                    step(dve.scalar_tensor_tensor(by_tile(w), by_tile(w), ROUTE_SCALE, bc(tot, NE), ALU.mult, ALU.mult))
                    step(dve.tensor_copy(comb_hl[:, :, 0:NE], by_tile(w)))
                    step(dve.tensor_tensor(comb_hl[:, :, NE:2 * NE], by_tile(w), comb_hl[:, :, 0:NE].bitcast(F32), ALU.subtract))

            def compare(step, val, out, n, before):
                r = val.shape[1] // n
                v = val.rearrange("p (r e) -> p r e", e=n)
                mine, other = v.unsqueeze(3).to_broadcast([P, r, n, n]), v.unsqueeze(2).to_broadcast([P, r, n, n])
                gt, ge = (cmp[:, j, 0:r * n * n].rearrange("p (r e f) -> p r e f", e=n, f=n) for j in range(2))
                dve.tensor_tensor(gt, other, mine, ALU.is_gt)
                step(dve.tensor_tensor(ge, other, mine, ALU.is_ge))

            def combine(step, val, out, n, before):
                r = val.shape[1] // n
                gt, ge = (cmp[:, j, 0:r * n * n].rearrange("p (r f) -> p r f", r=r) for j in range(2))
                step(dve.tensor_tensor(ge, ge, before.unsqueeze(1).to_broadcast([P, r, n * n]), ALU.mult))
                step(dve.tensor_tensor(gt, gt, ge, ALU.max))

            def count(step, val, out, n, before):
                size = val.shape[1] * n
                step(dve.tensor_reduce(out, cmp[:, 0, 0:size].rearrange("p (r e) -> p r e", e=n), AX_X, ALU.add))

            def expert(c, u, own, following):
                for n, cn in gap_steps(u, 0, own, following):
                    prefix(n, cn)
                dve.wait_ge(silu, c * NU + u + 1)
                dve.wait_ge(u_mm, c * NU + u + 1)
                if u >= NBUF:
                    dve.wait_ge(h_lo, c * NU + u - NBUF + 1)
                dve.tensor_tensor(h_s[:, u % NBUF, :], sg[:, :], pu[:, u % 2, :], ALU.mult).then_inc(gated, 1)
                dve.wait_ge(gated, c * NU + u + 1)
                if u < NSH:
                    dve.sem_inc(weighted, 1)
                else:
                    dve.wait_ge(w_mm, c * NE + u - NSH + 1)
                    dve.tensor_tensor(h_s[:, u % NBUF, :], h_s[:, u % NBUF, :], pw[:, :], ALU.mult).then_inc(weighted, 1)
                for n, cn in gap_steps(u, 1, own, following):
                    prefix(n, cn)

            def finish(c, last=False):
                dve.wait_ge(down, NU * (c + 1))
                if last:
                    dve.wait_ge(stored, 16 * (NCH - 1))
                dve.tensor_copy(out_s[:, :, :], po[:, :, :]).then_inc(out_sb, 1)
                dve.wait_ge(out_sb, c + 1)
                dve.sem_inc(po_free, 1)

            dve.memset(rstd[:, 3, :], EPS)
            dve.memset(rstd[:, 1, :], -0.5).then_inc(consts, 1)
            dve.sem_inc(po_free, 1)
            dve.memset(rw_hl[:, :, :].bitcast(F32), 0.0).then_inc(consts, 1)
            dve.wait_ge(small_in, 64)
            dve.tensor_scalar(bq_s[:, :], col[:, C_BQ:C_BQ + KD], SCALE, None, ALU.mult)
            dve.tensor_scalar(bk_e[:, :], col[:, C_BK:C_BK + KD], even, None, ALU.mult)
            dve.tensor_tensor(pick[:, :], ident_s[0:2 * NE, 0:NE], ident_s[0:2 * NE, NE:2 * NE], ALU.add).then_inc(consts, 1)
            for s in range(STEPS):
                if s == 3:
                    dve.wait_ge(aw_h_done, 1)
                    dve.tensor_tensor(aw_l[:, :], aw_s[:, 0:W_R], aw_h[:, :].bitcast(F32), ALU.subtract).then_inc(aw_l_done, 1)
                if s == 7:
                    r = aw_s[:, W_R:W_END].rearrange("p (k e) -> p k e", k=KD)
                    dve.wait_ge(consts, 3)
                    dve.tensor_copy(rw_hl[:, :, 0:NE], r).then_inc(consts, 1)
                    dve.wait_ge(consts, 4)
                    dve.tensor_tensor(rw_hl[:, :, NE:2 * NE], r, rw_hl[:, :, 0:NE].bitcast(F32), ALU.subtract).then_inc(rw_done, 1)
                prefix(s, 0, first=True)
            for u in range(NU):
                expert(0, u, None, 1)
            finish(0)
            with dve.Fori(1, NCH - 1) as c:
                for u in range(NU):
                    expert(c, u, c, c + 1)
                finish(c)
            for u in range(NU):
                expert(NCH - 1, u, NCH - 1, None)
            finish(NCH - 1, last=True)

        @block.gpsimd
        def _(pool):
            def rsqrt(i, c):
                pool.wait_ge(ln_mv[i], c + 1)
                pool.tensor_tensor(rstd[:, 0, :], mv[:, :, 1], rstd[:, 3, :], ALU.add).then_inc(ln_var[i], 1)
                pool.wait_ge(ln_var[i], c + 1)
                pool.tensor_tensor(rstd[:, 2, :], rstd[:, 0, :], rstd[:, 1, :], ALU.pow).then_inc(ln_rs[i], 1)

            def prefix(s, c):
                if s == 1:
                    rsqrt(0, c)
                if s == 3:
                    pool.wait_ge(ln_xn[0], c + 1)
                    pool.tensor_tensor(hres[:, :, :], hres[:, :, :], row[:, D:2 * D].unsqueeze(1).to_broadcast([P, NT, D]), ALU.add)\
                        .then_inc(h0_bo, 1)
                if s == 11:
                    pool.wait_ge(sm_r01, c + 1)
                    pool.tensor_tensor(p32[:, :, SEQ:Q], sd[:, :, :], bc(rc[:, 2, :], SEQ), ALU.mult).then_inc(p_odd, 1)
                if s == 15:
                    rsqrt(1, c)

            def expert(c, u, own, following):
                for n, cn in gap_steps(u, 0, own, following):
                    prefix(n, cn)
                pool.wait_ge(h_hi, c * NU + u + 1)
                if u >= NBUF:
                    pool.wait_ge(down, c * NU + u - NBUF + 1)
                pool.tensor_tensor(hl[:, u % NBUF, :], h_s[:, u % NBUF, :], hh[:, u % NBUF, :].bitcast(F32), ALU.subtract).then_inc(h_lo, 1)
                for n, cn in gap_steps(u, 1, own, following):
                    prefix(n, cn)

            def split_low(u):
                pool.wait_ge(fw_h_done, u + 1)
                pool.tensor_tensor(ffn_l[:, u, :], stage[:, u % 2, :], ffn_h[:, u, :].bitcast(F32), ALU.subtract).then_inc(fw_l_done, 1)

            pool.wait_ge(consts, 1)
            pool.wait_ge(small_in, 64)
            for s in range(STEPS):
                prefix(s, 0)
                if 3 <= s < 3 + NU:
                    split_low(s - 3)
            for u in range(NU):
                expert(0, u, None, 1)
            with pool.Fori(1, NCH - 1) as c:
                for u in range(NU):
                    expert(c, u, c, c + 1)
            for u in range(NU):
                expert(NCH - 1, u, NCH - 1, None)


def kernel(**inputs):
    import numpy as np
    import concourse.bacc as bacc
    from concourse.bass_utils import run_bass_kernel_spmd

    g = {k: np.asarray(v) for k, v in inputs.items()}
    C, F, PER = g["L0_tok_conv_w"].shape
    x = g["x"].reshape(TOK, PER, C).transpose(2, 1, 0).reshape(P, TOK)
    emb = g["L0_tok_emb_w"].T.reshape(C // 2, P, D).transpose(1, 0, 2).reshape(P, -1)
    conv = np.zeros((P, C // 2, 2, PER), np.float32)
    for ch in range(C):
        conv[(ch % 2) * F:(ch % 2) * F + F, ch // 2, ch % 2] = g["L0_tok_conv_w"][ch]
    tok = np.concatenate([emb, conv.reshape(P, -1)], 1)

    def halves(w):
        return w.reshape(KD, P, -1).transpose(1, 0, 2).reshape(P, -1)

    twice = lambda a, axis: np.concatenate([a, a], axis)
    attn = np.concatenate([halves(g["L0_attn_Wq"]), halves(twice(g["L0_attn_Wl"], 1)), twice(g["L0_attn_Wk"], 0),
                           twice(g["L0_attn_Wv"], 0), halves(g["L0_attn_Wo"]), halves(g["L0_ffn_router_weight"].T)], 1)
    experts = []
    for e in range(NSH):
        s = slice(e * P, e * P + P)
        experts.append((g["L0_ffn_sh_gate_w"][s], g["L0_ffn_sh_up_w"][s], g["L0_ffn_sh_down_w"][:, s]))
    for e in range(NE):
        experts.append((g["L0_ffn_gate_w"][e], g["L0_ffn_up_w"][e], g["L0_ffn_down_w"][e]))
    ffn = np.stack([np.concatenate([halves(a.T), halves(b.T), d.T], 1) for a, b, d in experts])
    half = (np.arange(P) // SEQ) % 2
    cols = np.concatenate([g["L0_attn_bq"].reshape(KD, P).T, twice(g["L0_attn_bl"], 0)[:, None], g["L0_attn_bk"].reshape(KD, P).T,
                           g["L0_attn_bv"].reshape(KD, P).T, (half == 0)[:, None], (half == 1)[:, None]], 1)
    rows = np.concatenate([g["L0_tok_emb_b"], g["L0_attn_bo"], g["L0_ffn_e_bias"]])
    tri = np.concatenate([np.tril(np.ones((n, n)), -1).ravel() for n in (NE, NGRP)])
    arrays = {"x_t": x, "tok_w": tok, "attn_w": attn, "ffn_w": ffn, "cols": cols, "rows": np.broadcast_to(rows, (P, rows.size)),
              "tri": np.broadcast_to(tri, (P, tri.size)), "ident": np.eye(P)}
    arrays = {k: np.ascontiguousarray(a, dtype=np.float32) for k, a in arrays.items()}

    nc = bacc.Bacc("TRN2", target_bir_lowering=False, num_devices=1)
    args = [nc.dram_tensor(n, a.shape, F32, kind="ExternalInput").ap() for n, a in arrays.items()]
    out = nc.dram_tensor("out_t", (D, TOK), F32, kind="ExternalOutput").ap()
    tower(nc, *args, out.rearrange("(k p) n -> p k n", p=P))
    r = run_bass_kernel_spmd(nc, [arrays], core_ids=[0])
    return np.ascontiguousarray(r.results[0]["out_t"].T).reshape(TOK // SEQ, SEQ, D)
```

```python
from contextlib import ExitStack
from typing import NamedTuple

import concourse.bass as bass
from concourse import mybir

F32 = mybir.dt.float32
F32R = mybir.dt.float32r
ALU = mybir.AluOpType
ACT = mybir.ActivationFunctionType
AX_X = mybir.AxisListType.X

P = 128
TOK = 2048
SEQ = 16
D = 256
KD = D // P
CH = 512
NCH = TOK // CH
BT = 512 // D
NT = CH // P
Q = 32
NQ = P // Q
NB = 2 * NQ * NT * 2
NE = 16
NSH = 2
NU = NE + NSH
NBUF = 3
LAG = 2
RING = 4
NGRP, TOPG, TOPK = 4, 2, 4
EPG = NE // NGRP
SCALE = 16 ** -0.5
ROUTE_SCALE = 2.5
EPS = 1e-5

C_BQ, C_BL, C_BK, C_BV, C_EVEN, C_ODD, NCOL = 0, 2, 3, 5, 7, 8, 9
W_Q, W_L, W_K, W_V, W_O, W_R, W_END = 0, 512, 768, 1024, 1280, 1792, 1824
ROUTE_OPS = 21
ROUTE_STEP = 22
ROUTE_AT = (0, 1, 14)
BIG = 3.4028234e38

ALONE = [0, 1, 2, 3, 4, 5, 6, 7, 7.5, 8, 9, 10, 11, 11.5, 12, 13, 14, 15, 15.5, 16, 16.5, 17, 18, 19, 20, 21]
OWN_FIRST = {23: 0, 24: 1, 25: 4}
OWN = {24: 1, 25: 3}
NEXT = {0: 5, 1: 6, 2: 8, 3: 9, 4: 11, 5: 12, 6: 13, 7: 15, 7.5: 16, 8: 17, 9: 18, 10: 19, 11: 20, 11.5: 18, 12: 20,
        13: 21, 14: 22, 15: 23, 15.5: 22, 16: 24, 16.5: 25, 17: 26, 18: 28, 19: 29, 20: 31, 21: 33, 22: 34, 23: 35}
SPLIT_HIGH = {4: 2, 5: 2, 8: 3, 10: 2, 13: 1, 16: 2, 17: 1, 18: 2, 20: 3}
SPLIT_LOW = {4: 2, 5: 3, 10: 2, 11.5: 3, 16: 4, 20: 4}


class Part(NamedTuple):
    c: int
    v: int
    t0: int
    nt: int
    first: bool = False


def whole(c):
    return Part(c, c + 1, 0, NT)


HALVES = [Part(0, h, h * BT, BT, True) for h in range(2)]


def alone():
    for i in range(len(ALONE) + 1):
        for h in (1, 0):
            if 0 <= i - h < len(ALONE):
                yield ALONE[i - h], HALVES[h]
    yield ROUTE_STEP, whole(0)


def splits(table, s, x):
    if x.t0:
        return range(0)
    before = sum(n for at, n in table.items() if at < s)
    return range(before, before + table.get(s, 0))


def gap_steps(u, side, own, following, first=False):
    g = 2 * u + side
    return [(n, own) for n, at in (OWN_FIRST if first else OWN).items() if at == g] + \
           [(n, following) for n, at in NEXT.items() if at == g and following is not None]


def tower(nc, x_t, tok_w, attn_w, ffn_w, cols, rows, tri, ident, out_t, comb_d):
    at = {"end": (nc.sbuf_base + 63) // 64 * 64}

    def sb(name, shape, dt=F32, over=None):
        size = 4
        for n in shape[1:]:
            size *= n
        start = at[over] if over else at["end"]
        at[name] = start
        if not over:
            at["end"] += (size + 31) // 32 * 32
        assert start + size <= nc.sbuf_usable_end, (name, start, size)
        return nc.alloc_sbuf_tensor_at(name, shape, dt, offset=start)

    with ExitStack() as ctx:
        def sem(name):
            return ctx.enter_context(nc.semaphore(name))

        def pair(name):
            return sem(name + "0"), sem(name + "1")

        def psum(name, shape):
            return ctx.enter_context(nc.psum_tensor(name, shape, F32))

        ffn_h = sb("ffn_h", [P, NU, 3 * D], F32R)
        ffn_l = sb("ffn_l", [P, NU, 3 * D], F32R)
        aw_h = sb("aw_h", [P, W_R], F32R)
        aw_l = sb("aw_l", [P, W_R], F32R)
        rw_hl = sb("rw_hl", [P, KD, P], F32R)
        w_tok = sb("w_tok", [P, D])
        ident_s = sb("ident_s", [P, P])
        col = sb("col", [P, NCOL])
        bq_s = sb("bq_s", [P, KD])
        bk_e = sb("bk_e", [P, KD])
        row = sb("row", [P, 2 * D + NE])
        tri_s = sb("tri_s", [P, NGRP * NGRP])
        even, odd = col[:, C_EVEN:C_EVEN + 1], col[:, C_ODD:C_ODD + 1]

        x_s = sb("x_s", [P, CH])
        hres = sb("hres", [P, NT, D])
        q_t = sb("q_t", [P, KD, CH])
        out_s = sb("out_s", [P, KD, CH], over="q_t")
        v_s = sb("v_s", [P, NT, D])
        xn = sb("xn", [P, NT, D])
        s1 = sb("s1", [P, CH], F32R, over="xn")
        sd = sb("sd", [P, NB, SEQ], over="xn")
        of = sb("of", [P, KD, CH], over="xn")
        keo = sb("keo", [P, KD, 2, CH])
        pt = sb("pt", [P, NB, Q], over="keo")
        emb_s = sb("emb_s", [P, 4 * (D + Q)], over="keo")
        xnt = sb("xnt", [P, 2, KD, CH], F32R)
        oht = sb("oht", [P, KD, 2, CH], F32R, over="xnt")
        p32 = sb("p32", [P, NB, Q], over="xnt")
        tmp = sb("tmp", [P, CH])
        xn2 = sb("xn2", [P, 2, 2, KD, CH], F32R)
        comb_t = sb("comb_t", [NE, CH], over="tmp")
        comb = sb("comb", [P, NT, Q])
        wts = sb("wts", [P, 2, CH])
        bn = sb("bn", [P, NT, 6])
        mv = sb("mv", [P, NT, 2])
        rstd = sb("rstd", [P, 4, NT])
        mx = sb("mx", [P, NB])
        rc = sb("rc", [P, 3, NB])
        rt = sb("rt", [P, 4, NT * NE])
        rg = sb("rg", [P, 10, NT * NGRP])
        cmp = sb("cmp", [P, 2, NT * NGRP * NGRP])
        masked = sb("masked", [P, NT, NE + 8])
        top = sb("top", [P, NT, 8])
        found = sb("found", [P, NT, NE + 8])
        sg = sb("sg", [P, CH])
        h_s = sb("h_s", [P, NBUF, CH])
        hh = sb("hh", [P, NBUF, CH], F32R)
        hl = sb("hl", [P, NBUF, CH], F32R)
        aw_s = sb("aw_s", [P, W_END], over="h_s")
        at["stage_a"], at["stage_b"] = at["xn2"] + 2 * KD * CH * 4, at["hl"]
        stages = [sb(name, [P, 2, 3 * D], over=name) for name in ("stage_a", "stage_b")]

        pre = psum("pre", [P, 2, 512])
        pg = psum("pg", [P, 2, 512])
        pu = psum("pu", [P, 2, 512])
        po = psum("po", [P, KD, 512])

        def pair_of_banks(m, x):
            if x.first:
                return ((pre, po), (pu, pg))[m][x.t0 // BT]
            return pre

        def bank(name, x):
            first = {"lat": (0, 0), "q0": (0, 1), "q1": (1, 0), "k0": (1, 1), "k1": (0, 0)}
            m, b = (first if x.first else {"lat": (0, 0), "q0": (0, 1), "q1": (0, 0), "k0": (0, 1), "k1": (0, 0)})[name]
            return pair_of_banks(m, x)[:, b, 0:x.nt * P]

        def token_major(x, b=0):
            return pair_of_banks(0, x)[:, :, :].rearrange("p b (t d) -> p (b t) d", d=D)[:, b * BT:b * BT + x.nt, :]

        def blocks(m, x):
            banks = pair_of_banks(1 - m, x)
            return banks[:, :, :].rearrange("p b (n j) -> p (b n) j", j=Q)[:, 0::NT // x.nt, :]

        def block_of(m, x):
            return m * NB // 2 + x.t0 * 2 * NQ

        def these(m, x):
            return slice(block_of(m, x), block_of(m, x) + x.nt * 2 * NQ)

        tok_in, small_in, aw_in, x_in = sem("tok_in"), sem("small_in"), sem("aw_in"), sem("x_in")
        ffn_in = [sem(f"ffn_in{i}") for i in range(RING)]
        consts, wtok_mm, wtok_done = sem("consts"), sem("wtok_mm"), sem("wtok_done")
        aw_h_done, aw_l_done, rw_done = sem("aw_h_done"), sem("aw_l_done"), sem("rw_done")
        fw_h_done, fw_l_done = sem("fw_h_done"), sem("fw_l_done")
        h0_mm, h0_sum, h0_done, h0_bo = sem("h0_mm"), sem("h0_sum"), sem("h0_done"), sem("h0_bo")
        ln_bn, ln_mv, ln_var, ln_rs, ln_xn = (pair(x) for x in ("ln_bn", "ln_mv", "ln_var", "ln_rs", "ln_xn"))
        xn_tr, xn_hi, xn_lo = pair("xn_tr"), pair("xn_hi"), pair("xn_lo")
        q_mm, q_done = pair("q_mm"), pair("q_done")
        lat_mm, lat_f, lat_h, lat_l = (sem(x) for x in ("lat_mm", "lat_f", "lat_h", "lat_l"))
        v_mm, v_done = sem("v_mm"), sem("v_done")
        k_mm, k_even, k_odd = pair("k_mm"), pair("k_even"), pair("k_odd")
        sc_mm, sc_t, sc_done = pair("sc_mm"), pair("sc_t"), pair("sc_done")
        sc_row, pv_row = pair("sc_row"), pair("pv_row")
        sm_max, sm_sub, sm_exp, sm_sum, sm_rc, sm_r01 = (pair(x) for x in ("sm_max", "sm_sub", "sm_exp", "sm_sum", "sm_rc", "sm_r01"))
        p_even, p_odd, pt_done = pair("p_even"), pair("p_odd"), pair("pt_done")
        pv_mm, pv_t, o_done, o_hi, o_lo = (pair(x) for x in ("pv_mm", "pv_t", "o_done", "o_hi", "o_lo"))
        wo_mm, h1_done = sem("wo_mm"), sem("h1_done")
        lg_mm, lg_sb, lg_tr, lg_tok, lg_exp = (sem(x) for x in ("lg_mm", "lg_sb", "lg_tr", "lg_tok", "lg_exp"))
        route = sem("route")
        top_done, comb_tr, comb_done = sem("top_done"), sem("comb_tr"), sem("comb_done")
        res_mm = sem("res_mm")
        g_mm, u_mm = sem("g_mm"), sem("u_mm")
        silu, gated, weighted, h_hi, h_lo = sem("silu"), sem("gated"), sem("weighted"), sem("h_hi"), sem("h_lo")
        down = sem("down")
        comb_stored, wts_in = sem("comb_stored"), pair("wts_in")
        po_free = sem("po_free")
        out_sb, stored = sem("out_sb"), sem("stored")

        block = ctx.enter_context(nc.Block())

        def par(c):
            return c % 2

        def bc(ap, n):
            return ap.unsqueeze(len(ap.shape)).to_broadcast([*ap.shape, n])

        def stage(u):
            return stages[u % RING // 2][:, u % 2, :]

        def value(eng, n):
            return n if isinstance(n, int) else eng.snap(n)

        def grouped(ap, nt):
            return ap.rearrange("p (b t n) -> p b t n", b=NQ, t=nt)

        def by_group(ap, nt):
            return ap.rearrange("p (t b n) -> p b t n", b=NQ, t=nt)

        @block.sync
        def _(sp):
            def load_expert(u):
                if u >= RING:
                    sp.wait_ge(fw_h_done, u - RING + 1)
                    sp.wait_ge(fw_l_done, u - RING + 1)
                sp.dma_start(stage(u), ffn_w[u]).then_inc(ffn_in[u % RING], 16)

            def load_x(c):
                sp.wait_ge(h0_mm, 2 * c)
                sp.dma_start(x_s[:, :], x_t[:, bass.ds(c * CH, CH)]).then_inc(x_in, 16)

            def store(c):
                sp.wait_ge(out_sb, c + 1)
                sp.dma_start(out_t[:, :, bass.ds(c * CH, CH)], out_s[:, :, :]).then_inc(stored, 16)

            def spread_weights(c, first=False, ahead=True):
                sp.wait_ge(comb_done, c + 1)
                sp.dma_start(comb_d, comb_t[:, :]).then_inc(comb_stored, 16)
                sp.wait_ge(comb_stored, 16 * (c + 1))
                for e in range(NE):
                    if e >= 2 or not first:
                        sp.wait_ge(weighted, c * NU + (NSH + e - 1 if e >= 2 else e - 1))
                    sp.dma_start(wts[:, e % 2, :], comb_d[e:e + 1, :].to_broadcast([P, CH])).then_inc(wts_in[e % 2], 16)
                    if e == 2 and not first:
                        store(c - 1)
                    if e == 4 and ahead:
                        load_x(c + 2)

            sp.dma_start(emb_s[:, :], tok_w).then_inc(tok_in, 16)
            sp.dma_start(x_s[:, :], x_t[:, 0:CH]).then_inc(x_in, 16)
            sp.dma_start(col[:, :], cols).then_inc(small_in, 16)
            sp.dma_start(row[:, :], rows).then_inc(small_in, 16)
            sp.dma_start(ident_s[:, :], ident).then_inc(small_in, 16)
            sp.dma_start(tri_s[:, :], tri).then_inc(small_in, 16)
            sp.dma_start(aw_s[:, :], attn_w).then_inc(aw_in, 16)
            load_x(1)
            for u in range(NU):
                load_expert(u)
            spread_weights(0, first=True)
            with sp.Fori(1, NCH - 2) as c:
                spread_weights(c)
            spread_weights(NCH - 2, ahead=False)
            spread_weights(NCH - 1, ahead=False)
            store(NCH - 1)
            sp.wait_ge(stored, 16 * NCH)

        @block.tensor
        def _(pe):
            def split_mm(out, w_at, x_at):
                i, n = 0, 3 * KD
                for k in range(KD):
                    for a, b in ((0, 0), (0, 1), (1, 0)):
                        last = pe.matmul(out, w_at(a, k), x_at(b, k), start=i == 0, stop=i == n - 1)
                        i += 1
                return last

            def transpose_xn(i, x):
                for k in range(KD):
                    for t in range(x.nt):
                        last = pe.transpose(pair_of_banks(0, x)[:, k, t * P:(t + 1) * P], xn[:, x.t0 + t, k * P:(k + 1) * P], ident_s[:, :])
                    last.then_inc(xn_tr[i], 1)

            def project(out, w0, stride, cols):
                return split_mm(out, lambda a, k: (aw_h, aw_l)[a][:, w0 + k * stride:w0 + k * stride + P],
                                lambda b, k: xnt[:, b, k, cols])

            def k_half(m, out, cols):
                for i, w in enumerate((aw_h, aw_l)):
                    last = pe.matmul(out, w[:, W_K + m * P:W_K + m * P + P], s1[:, cols], start=i == 0, stop=i == 1)
                last.then_inc(k_mm[m], 1)

            def prefix(s, x):
                c, v, t0, nt, first = x
                cols, tiles = slice(t0 * P, (t0 + nt) * P), slice(t0, t0 + nt)
                if s == 0:
                    pe.wait_ge(x_in, 16 * c + 16)
                    if not first:
                        pe.wait_ge(comb_done, c)
                    for t in range(nt):
                        last = pe.matmul(token_major(x)[:, t, :], x_s[:, (t0 + t) * P:(t0 + t + 1) * P], w_tok[:, :], start=True, stop=True)
                        if t % BT == BT - 1:
                            last.then_inc(h0_mm, 1)
                if s == 3:
                    pe.wait_ge(ln_xn[0], v + 1)
                    transpose_xn(0, x)
                if s == 4:
                    pe.wait_ge(xn_hi[0], KD * (v + 1))
                    pe.wait_ge(xn_lo[0], KD * (v + 1))
                    project(bank("lat", x), W_L, P, cols).then_inc(lat_mm, 1)
                    project(bank("q0", x), W_Q, D, cols).then_inc(q_mm[0], 1)
                if s == 5:
                    if not first:
                        pe.wait_ge(lat_f, v + 1)
                    project(bank("q1", x), W_Q + P, D, cols).then_inc(q_mm[1], 1)
                    pe.wait_ge(lat_l, v + 1)
                    if not first:
                        pe.wait_ge(q_done[0], v + 1)
                    k_half(0, bank("k0", x), cols)
                if s == 6:
                    if not first:
                        pe.wait_ge(q_done[1], v + 1)
                    k_half(1, bank("k1", x), cols)
                if s == 7:
                    if not first:
                        for m in range(KD):
                            pe.wait_ge(k_even[m], v + 1)
                    else:
                        pe.wait_ge(q_done[0], v + 1)
                    for t in range(nt):
                        for i, w in enumerate((aw_h, aw_l)):
                            last = pe.matmul(token_major(x, int(first))[:, t, :], s1[:, (t0 + t) * P:(t0 + t + 1) * P], w[:, W_V:W_V + D],
                                             start=i == 0, stop=i == 1)
                    last.then_inc(v_mm, 1)
                if s in (7.5, 8, 11.5, 12):
                    m = int(s > 11)
                    n = value(pe, v + 1)
                    pe.wait_ge(tok_in, 16)
                    if s in (8, 12):
                        pass
                    elif first:
                        pe.wait_ge(k_even[0] if m == 0 else v_done, n)
                    else:
                        pe.wait_ge(v_done if m == 0 else sc_done[0], n)
                    out = blocks(m, x).rearrange("p (g t h) j -> p g t h j", g=NQ, t=nt)
                    if s in (8, 12):
                        pe.wait_ge(sc_row[m], n)
                    for t in range(nt):
                        for b in range(NQ):
                            tok = slice((t0 + t) * P + b * Q, (t0 + t) * P + b * Q + Q)
                            for g in (1, 3) if s in (8, 12) else (0, 2):
                                rows_g = slice(g * Q, g * Q + Q)
                                last = pe.matmul(out[b * Q:b * Q + Q, g, t], q_t[rows_g, m, tok], keo[rows_g, m, :, tok],
                                                 start=True, stop=True, tile_position=(g * Q, b * Q))
                    last.then_inc((sc_mm if s in (8, 12) else sc_row)[m], 1)
                if s in (15.5, 16, 16.5, 17):
                    m = int(s > 16)
                    n = value(pe, v + 1)
                    pe.wait_ge(tok_in, 16)
                    pe.wait_ge(pt_done[m], n)
                    if not first and s in (15.5, 16.5):
                        pe.wait_ge(sc_done[1] if m == 0 else o_done[0], n)
                    out = blocks(m, x).rearrange("p (g t h) j -> p g t h j", g=NQ, t=nt)
                    if s in (16, 17):
                        pe.wait_ge(pv_row[m], n)
                    for t in range(nt):
                        for g in range(NQ):
                            blk = block_of(m, x) + (g * nt + t) * 2
                            for b in (1, 3) if s in (16, 17) else (0, 2):
                                rows_b = slice(b * Q, b * Q + Q)
                                last = pe.matmul(out[g * Q:g * Q + Q, b, t], v_s[rows_b, t0 + t, m * P + g * Q:m * P + g * Q + Q],
                                                 pt[rows_b, blk:blk + 2, :], start=True, stop=True, tile_position=(b * Q, g * Q))
                    last.then_inc((pv_mm if s in (16, 17) else pv_row)[m], 1)
                if s == 18:
                    for m in range(KD):
                        pe.wait_ge(o_hi[m], v + 1)
                        pe.wait_ge(o_lo[m], v + 1)
                    for t in range(nt):
                        last = split_mm(token_major(x)[:, t, :], lambda a, m: oht[:, m, a, (t0 + t) * P:(t0 + t + 1) * P],
                                        lambda b, m: (aw_h, aw_l)[b][:, W_O + m * D:W_O + m * D + D])
                        if t % BT == BT - 1:
                            last.then_inc(wo_mm, 1)
                if s == 20:
                    pe.wait_ge(ln_xn[1], v + 1)
                    transpose_xn(1, x)
                if s == 21:
                    pe.wait_ge(xn_hi[1], KD * (v + 1))
                    pe.wait_ge(xn_lo[1], KD * (v + 1))
                    if first:
                        pe.wait_ge(rw_done, 1)
                    for i in range(2 * KD):
                        last = pe.matmul(pair_of_banks(0, x)[:, 0, 0:nt * P], rw_hl[:, i % KD, :], xn2[:, par(c), i // KD, i % KD, cols],
                                         start=i == 0, stop=i == 2 * KD - 1)
                    last.then_inc(lg_mm, 1)
                if s == 22:
                    n = value(pe, c + 2)
                    pe.wait_ge(tok_in, 16)
                    pe.wait_ge(lg_sb, n)
                    for t in range(NT):
                        last = pe.transpose(pre[:, 1, t * 2 * NE:(t + 1) * 2 * NE], tmp[0:2 * NE, t * P:(t + 1) * P],
                                            ident_s[0:2 * NE, 0:2 * NE])
                    last.then_inc(lg_tr, 1)
                if s == 25:
                    n = value(pe, ROUTE_OPS * (c + 1))
                    pe.wait_ge(tok_in, 16)
                    pe.wait_ge(route, n)
                    for t in range(NT):
                        last = pe.transpose(pre[0:Q, 0, t * P:(t + 1) * P], comb[:, t, :], ident_s[:, :])
                    last.then_inc(comb_tr, 1)

            def residual(c, first):
                if not first:
                    pe.wait_ge(po_free, c)
                pe.wait_ge(h1_done, c + 2)
                for k in range(KD):
                    for t in range(NT):
                        last = pe.matmul(po[:, k, t * P:(t + 1) * P], hres[:, t, k * P:(k + 1) * P], ident_s[:, :],
                                         is_transpose=True, start=t == 0, stop=False, skip_group_check=True)
                last.then_inc(res_mm, 1)

            def ffn_mm(c, u, out, off):
                return split_mm(out, lambda a, k: (ffn_h, ffn_l)[a][:, u, off + k * P:off + k * P + P],
                                lambda b, k: xn2[:, par(c), b, k, :])

            def expert(c, u, following, first=False):
                if first:
                    pe.wait_ge(fw_l_done, u + 1)
                if u > 1 or not first:
                    pe.wait_ge(silu, c * NU + u - 1)
                ffn_mm(c, u, pg[:, u % 2, :], 0).then_inc(g_mm, 1)
                for n, cn in gap_steps(u, 0, c, following, first):
                    prefix(n, whole(cn))
                if u > 1 or not first:
                    pe.wait_ge(gated, c * NU + u - 1)
                ffn_mm(c, u, pu[:, u % 2, :], D).then_inc(u_mm, 1)
                if u == LAG:
                    residual(c, first)
                if u >= LAG:
                    down_mm(c * NU + u - LAG, u - LAG)
                elif not first:
                    down_mm(c * NU + u - LAG, NU + u - LAG)
                for n, cn in gap_steps(u, 1, c, following, first):
                    prefix(n, whole(cn))

            def down_mm(n, u):
                pe.wait_ge(h_lo, n + 1)
                for k in range(KD):
                    for i, (w, x) in enumerate(((ffn_h, hh), (ffn_h, hl), (ffn_l, hh))):
                        last = pe.matmul(po[:, k, :], w[:, u, 2 * D + k * P:2 * D + k * P + P], x[:, u % NBUF, :],
                                         start=False, stop=u == NU - 1 and i == 2, skip_group_check=True)
                last.then_inc(down, 1)

            pe.wait_ge(tok_in, 16)
            for i in range(4):
                last = pe.matmul(pre[i * Q:i * Q + Q, 0, 0:D], emb_s[:, 4 * D + i * Q:4 * D + i * Q + Q], emb_s[:, i * D:i * D + D],
                                 start=True, stop=True)
            last.then_inc(wtok_mm, 1)
            pe.wait_ge(wtok_done, 1)
            pe.wait_ge(small_in, 64)
            for s, x in alone():
                if s in (4, 5):
                    pe.wait_ge(aw_h_done, 1)
                    pe.wait_ge(aw_l_done, s - 3)
                prefix(s, x)
            for u in range(NU):
                expert(0, u, 1, first=True)
            with pe.Fori(1, NCH - 1) as c:
                for u in range(NU):
                    expert(c, u, c + 1)
            for u in range(NU):
                expert(NCH - 1, u, None)
            for u in range(NU - LAG, NU):
                down_mm((NCH - 1) * NU + u, u)

        @block.scalar
        def _(act):
            def prefix(s, x, early=False):
                c, v, t0, nt, first = x
                cols, tiles = slice(t0 * P, (t0 + nt) * P), slice(t0, t0 + nt)
                if s in (3, 20):
                    i = int(s == 20)
                    if early and i == 1:
                        act.wait_ge(fw_l_done, NU)
                    dst = xnt[:, 0, :, cols] if i == 0 else xn2[:, par(c), 0, :, cols]
                    for k in range(KD):
                        act.wait_ge(xn_tr[i], KD * v + k + 1)
                        act.activation(dst[:, k, :], pair_of_banks(0, x)[:, k, 0:nt * P], ACT.Copy).then_inc(xn_hi[i], 1)
                if s == 4:
                    act.wait_ge(lat_f, v + 1)
                    act.activation(s1[:, cols], tmp[:, cols], ACT.Copy).then_inc(lat_h, 1)
                    if not (first or early):
                        act.wait_ge(stored, 16 * (c - 1))
                if s in (4, 5):
                    m = s - 4
                    act.wait_ge(q_mm[m], v + 1)
                    act.activation(q_t[:, m, cols], bank(f"q{m}", x), ACT.Identity, bias=bq_s[:, m:m + 1], scale=SCALE).then_inc(q_done[m], 1)
                if s in (5, 6):
                    m = s - 5
                    act.wait_ge(k_odd[m], v + 1)
                    act.activation(keo[:, m, 0, cols], bank(f"k{m}", x), ACT.Identity, bias=bk_e[:, m:m + 1], scale=even).then_inc(k_even[m], 1)
                if s == 7:
                    act.wait_ge(v_mm, v + 1)
                    act.activation(v_s[:, tiles, :], token_major(x, int(first)), ACT.Copy).then_inc(v_done, 1)
                if s in (8, 12):
                    m = int(s == 12)
                    act.wait_ge(sc_mm[m], v + 1)
                    if m == 1:
                        act.wait_ge(sc_done[0], v + 1)
                    act.activation(tmp[:, cols].rearrange("p (n j) -> p n j", j=SEQ), blocks(m, x)[:, :, 0:SEQ], ACT.Identity, bias=0.0, scale=even)\
                       .then_inc(sc_t[m], 1)
                if s in (9, 13):
                    m = int(s == 13)
                    act.wait_ge(sm_sub[m], v + 1)
                    act.activation(sd[:, these(m, x), :], sd[:, these(m, x), :], ACT.Exp).then_inc(sm_exp[m], 1)
                if s in (16, 17):
                    m = s - 16
                    act.wait_ge(pv_mm[m], v + 1)
                    if m == 1:
                        act.wait_ge(o_lo[0], v + 1)
                    act.activation(tmp[:, cols].rearrange("p (n j) -> p n j", j=Q), blocks(m, x)[:, 1::2, :], ACT.Identity,
                                   bias=col[:, C_BV + m:C_BV + m + 1], scale=odd).then_inc(pv_t[m], 1)
                    act.wait_ge(o_done[m], v + 1)
                    act.activation(by_group(oht[:, m, 0, cols], nt), grouped(of[:, m, cols], nt), ACT.Copy).then_inc(o_hi[m], 1)
                if s == 21:
                    act.wait_ge(lg_mm, v + 1)
                    act.activation(tmp[0:2 * NE, cols], pair_of_banks(0, x)[0:2 * NE, 0, 0:nt * P], ACT.Copy).then_inc(lg_sb, 1)
                if s == 22:
                    act.wait_ge(lg_tr, c + 1)
                    act.activation(rt[:, 0:2, :].rearrange("p a n -> p (a n)"), pre[:, 1, 0:NT * 2 * NE], ACT.Copy).then_inc(lg_tok, 1)
                    act.wait_ge(route, ROUTE_OPS * c + 1)
                    act.activation(rt[:, 3, :], rt[:, 2, :], ACT.Exp, scale=-1.0).then_inc(lg_exp, 1)
                if s == 25:
                    act.wait_ge(comb_tr, c + 1)
                    act.activation(comb_t[:, :], pre[0:NE, 0, :], ACT.Copy).then_inc(comb_done, 1)

            def finish(c, last=False):
                act.wait_ge(down, NU * (c + 1))
                if last:
                    act.wait_ge(stored, 16 * (NCH - 1))
                act.activation(out_s[:, :, :], po[:, :, :], ACT.Copy).then_inc(out_sb, 1)
                act.wait_ge(out_sb, c + 1)
                act.sem_inc(po_free, 1)

            def expert(c, u, following, first=False):
                if u == LAG and not first:
                    finish(c - 1)
                act.wait_ge(g_mm, c * NU + u + 1)
                if u > 0 or not first:
                    act.wait_ge(gated, c * NU + u)
                act.activation(sg[:, :], pg[:, u % 2, :], ACT.Silu).then_inc(silu, 1)
                for n, cn in gap_steps(u, 0, c, following, first):
                    prefix(n, whole(cn), early=first)
                act.wait_ge(weighted, c * NU + u + 1)
                if u >= NBUF or not first:
                    act.wait_ge(down, c * NU + u - NBUF + 1)
                act.activation(hh[:, u % NBUF, :], h_s[:, u % NBUF, :], ACT.Copy).then_inc(h_hi, 1)
                for n, cn in gap_steps(u, 1, c, following, first):
                    prefix(n, whole(cn), early=first)

            def split_high(u):
                act.wait_ge(ffn_in[u % RING], 16 * (u // RING + 1))
                act.activation(ffn_h[:, u, :], stage(u), ACT.Copy).then_inc(fw_h_done, 1)

            act.wait_ge(wtok_mm, 1)
            act.activation(w_tok[:, :], pre[:, 0, 0:D], ACT.Copy).then_inc(wtok_done, 1)
            act.wait_ge(aw_in, 16)
            act.activation(aw_h[:, :], aw_s[:, 0:W_R], ACT.Copy).then_inc(aw_h_done, 1)
            for s, x in alone():
                for u in splits(SPLIT_HIGH, s, x):
                    split_high(u)
                prefix(s, x)
            for u in range(NU):
                expert(0, u, 1, first=True)
            with act.Fori(1, NCH - 1) as c:
                for u in range(NU):
                    expert(c, u, c + 1)
            for u in range(NU):
                expert(NCH - 1, u, None)
            finish(NCH - 1, last=True)

        @block.vector
        def _(dve):
            def norm_stats(i, x):
                for t in range(x.t0, x.t0 + x.nt):
                    last = dve.bn_stats(bn[:, t, :], hres[:, t, :])
                last.then_inc(ln_bn[i], 1)
                n = value(dve, x.v + 1)
                dve.wait_ge(small_in, 64)
                dve.wait_ge(ln_bn[i], n)
                for t in range(x.t0, x.t0 + x.nt):
                    last = dve.bn_aggr(mv[:, t, :], bn[:, t, :])
                last.then_inc(ln_mv[i], 1)

            def norm_apply(i, x):
                dve.wait_ge(ln_rs[i], x.v + 1)
                for t in range(x.t0, x.t0 + x.nt):
                    last = dve.tensor_scalar(xn[:, t, :], hres[:, t, :], mv[:, t, 0:1], rstd[:, 2, t:t + 1], ALU.subtract, ALU.mult)
                last.then_inc(ln_xn[i], 1)

            def prefix(s, x):
                c, v, t0, nt, first = x
                cols, tiles = slice(t0 * P, (t0 + nt) * P), slice(t0, t0 + nt)
                if s == 0:
                    if not first:
                        dve.wait_ge(res_mm, c)
                    for b in range(nt // BT):
                        tiles, there = slice(t0 + b * BT, t0 + b * BT + BT), slice(b * BT, b * BT + BT)
                        dve.wait_ge(h0_mm, 2 * c + t0 // BT + b + 1)
                        dve.tensor_tensor(hres[:, tiles, :], token_major(x)[:, there, :], row[:, 0:D].unsqueeze(1).to_broadcast([P, BT, D]), ALU.add)\
                           .then_inc(h0_sum, 1)
                    for b in range(nt // BT):
                        tiles = slice(t0 + b * BT, t0 + b * BT + BT)
                        dve.wait_ge(h0_sum, 2 * c + t0 // BT + b + 1)
                        last = dve.tensor_scalar(hres[:, tiles, :], hres[:, tiles, :], 0.0, None, ALU.max)
                    last.then_inc(h0_done, 1)
                if s == 1:
                    dve.wait_ge(h0_done, v + 1)
                    norm_stats(0, x)
                if s == 2:
                    norm_apply(0, x)
                if s in (3, 20):
                    i = int(s == 20)
                    hi, lo = (xnt[:, j, :, cols] if i == 0 else xn2[:, par(c), j, :, cols] for j in range(2))
                    for k in range(KD):
                        dve.wait_ge(xn_hi[i], KD * v + k + 1)
                        dve.tensor_tensor(lo[:, k, :], pair_of_banks(0, x)[:, k, 0:nt * P], hi[:, k, :].bitcast(F32), ALU.subtract).then_inc(xn_lo[i], 1)
                if s == 4:
                    dve.wait_ge(lat_mm, v + 1)
                    if not first:
                        dve.wait_ge(comb_stored, 16 * c)
                    dve.tensor_scalar(tmp[:, cols], bank("lat", x), col[:, C_BL:C_BL + 1], None, ALU.add).then_inc(lat_f, 1)
                    dve.wait_ge(lat_h, v + 1)
                    dve.tensor_tensor(s1[64:128, cols], tmp[64:128, cols], s1[64:128, cols].bitcast(F32), ALU.subtract).then_inc(lat_l, 1)
                if s in (5, 6):
                    m = s - 5
                    dve.wait_ge(k_mm[m], v + 1)
                    dve.tensor_scalar(keo[:, m, 1, cols], bank(f"k{m}", x), col[:, C_BK + m:C_BK + m + 1], odd, ALU.add, ALU.mult).then_inc(k_odd[m], 1)
                if s in (8, 12):
                    m = int(s == 12)
                    dve.wait_ge(sc_t[m], v + 1)
                    dve.scalar_tensor_tensor(sd[:, these(m, x), :], blocks(m, x)[:, :, SEQ:Q], odd,
                                             tmp[:, cols].rearrange("p (n j) -> p n j", j=SEQ), ALU.mult, ALU.add).then_inc(sc_done[m], 1)
                if s in (9, 13):
                    m = int(s == 13)
                    half = these(m, x)
                    dve.wait_ge(sc_done[m], v + 1)
                    dve.tensor_reduce(mx[:, half], sd[:, half, :], AX_X, ALU.max).then_inc(sm_max[m], 1)
                    dve.wait_ge(sm_max[m], v + 1)
                    dve.tensor_tensor(sd[:, half, :], sd[:, half, :], bc(mx[:, half], SEQ), ALU.subtract).then_inc(sm_sub[m], 1)
                if s in (10, 14):
                    m = int(s == 14)
                    half = these(m, x)
                    dve.wait_ge(sm_exp[m], v + 1)
                    dve.tensor_reduce(rc[:, 0, half], sd[:, half, :], AX_X, ALU.add).then_inc(sm_sum[m], 1)
                    dve.wait_ge(sm_sum[m], v + 1)
                    dve.reciprocal(rc[:, 0, half], rc[:, 0, half]).then_inc(sm_rc[m], 1)
                    dve.wait_ge(sm_rc[m], v + 1)
                    dve.tensor_scalar(rc[:, 1, half], rc[:, 0, half], even, None, ALU.mult)
                    dve.tensor_scalar(rc[:, 2, half], rc[:, 0, half], odd, None, ALU.mult).then_inc(sm_r01[m], 1)
                    dve.wait_ge(sm_r01[m], v + 1)
                    dve.tensor_tensor(p32[:, half, 0:SEQ], sd[:, half, :], bc(rc[:, 1, half], SEQ), ALU.mult).then_inc(p_even[m], 1)
                if s in (11, 15):
                    m = int(s == 15)
                    half = these(m, x)
                    dve.wait_ge(p_even[m], v + 1)
                    dve.wait_ge(p_odd[m], v + 1)
                    dve.transpose(pt[:, half, :].rearrange("p n i -> p (n i)"), p32[:, half, :].rearrange("p n j -> p (n j)")).then_inc(pt_done[m], 1)
                if s in (16, 17):
                    m = s - 16
                    dve.wait_ge(pv_t[m], v + 1)
                    dve.scalar_tensor_tensor(of[:, m, cols].rearrange("p (n j) -> p n j", j=Q), blocks(m, x)[:, 0::2, :], even,
                                             tmp[:, cols].rearrange("p (n j) -> p n j", j=Q), ALU.mult, ALU.add).then_inc(o_done[m], 1)
                    dve.wait_ge(o_hi[m], v + 1)
                    dve.tensor_tensor(by_group(oht[:, m, 1, cols], nt), grouped(of[:, m, cols], nt), by_group(oht[:, m, 0, cols], nt).bitcast(F32),
                                      ALU.subtract).then_inc(o_lo[m], 1)
                if s == 18:
                    dve.wait_ge(h0_bo, v + 1)
                    for b in range(nt // BT):
                        tiles, there = slice(t0 + b * BT, t0 + b * BT + BT), slice(b * BT, b * BT + BT)
                        dve.wait_ge(wo_mm, 2 * c + t0 // BT + b + 1)
                        last = dve.tensor_tensor(hres[:, tiles, :], token_major(x)[:, there, :], hres[:, tiles, :], ALU.add)
                    last.then_inc(h1_done, 1)
                    dve.wait_ge(h1_done, v + 1)
                    norm_stats(1, x)
                if s == 19:
                    norm_apply(1, x)
                if s in range(ROUTE_STEP, ROUTE_STEP + 3):
                    routing(s, c)

            def routing(s, c):
                done = [ROUTE_OPS * c + ROUTE_AT[s - ROUTE_STEP]]

                def step(ins):
                    done[0] = done[0] + 1
                    ins.then_inc(route, 1)
                    dve.wait_ge(route, done[0])

                score, sc, w = rt[:, 3, :], rt[:, 2, :], rt[:, 2, :]

                def by_tile(ap):
                    return ap.rearrange("p (t e) -> p t e", t=NT)

                if s == 22:
                    z = rt[:, 0:2, :].rearrange("p a n -> p (a n)").rearrange("p (t a e) -> p t a e", t=NT, a=2)
                    dve.wait_ge(lg_tok, c + 1)
                    step(dve.tensor_tensor(by_tile(sc), z[:, :, 0, :], z[:, :, 1, :], ALU.add))
                if s == 23:
                    dve.wait_ge(lg_exp, c + 1)
                    step(dve.tensor_scalar(score, score, 1.0, None, ALU.add))
                    step(dve.reciprocal(score, score))
                    step(dve.tensor_tensor(by_tile(sc), by_tile(score), row[:, 2 * D:2 * D + NE].unsqueeze(1).to_broadcast([P, NT, NE]), ALU.add))
                    pairs = sc.rearrange("p (g a b) -> p g a b", a=2, b=2)
                    big, small = (rg[:, j:j + 2, :].rearrange("p a n -> p (a n)").rearrange("p (g a) -> p g a", a=2) for j in (0, 2))
                    dve.tensor_tensor(big, pairs[:, :, :, 0], pairs[:, :, :, 1], ALU.max)
                    step(dve.tensor_tensor(small, pairs[:, :, :, 0], pairs[:, :, :, 1], ALU.min))
                    dve.tensor_tensor(rg[:, 4, :], big[:, :, 0], big[:, :, 1], ALU.max)
                    dve.tensor_tensor(rg[:, 5, :], big[:, :, 0], big[:, :, 1], ALU.min)
                    step(dve.tensor_tensor(rg[:, 6, :], small[:, :, 0], small[:, :, 1], ALU.max))
                    step(dve.tensor_tensor(rg[:, 7, :], rg[:, 5, :], rg[:, 6, :], ALU.max))
                    step(dve.tensor_tensor(rg[:, 8, :], rg[:, 4, :], rg[:, 7, :], ALU.add))
                    v = rg[:, 8, :].rearrange("p (t g) -> p t g", t=NT)
                    mine, other = v.unsqueeze(3).to_broadcast([P, NT, NGRP, NGRP]), v.unsqueeze(2).to_broadcast([P, NT, NGRP, NGRP])
                    gt, ge = cmp[:, 0, :], cmp[:, 1, :]
                    dve.tensor_tensor(gt.rearrange("p (t g f) -> p t g f", g=NGRP, f=NGRP), other, mine, ALU.is_gt)
                    step(dve.tensor_tensor(ge.rearrange("p (t g f) -> p t g f", g=NGRP, f=NGRP), other, mine, ALU.is_ge))
                    step(dve.tensor_tensor(ge.rearrange("p (t f) -> p t f", t=NT), ge.rearrange("p (t f) -> p t f", t=NT),
                                           tri_s[:, :].unsqueeze(1).to_broadcast([P, NT, NGRP * NGRP]), ALU.mult))
                    step(dve.tensor_tensor(gt, gt, ge, ALU.max))
                    step(dve.tensor_reduce(rg[:, 9, :], gt.rearrange("p (g f) -> p g f", f=NGRP), AX_X, ALU.add))
                    step(dve.tensor_scalar(rg[:, 9, :], rg[:, 9, :], float(TOPG), None, ALU.is_lt))
                    step(dve.tensor_tensor(masked[:, :, 0:NE].rearrange("p t (g a) -> p t g a", a=EPG),
                                           sc.rearrange("p (t g a) -> p t g a", t=NT, a=EPG),
                                           bc(rg[:, 9, :].rearrange("p (t g) -> p t g", t=NT), EPG), ALU.mult))
                if s == 24:
                    for t in range(NT):
                        last = dve.max(top[:, t, :], masked[:, t, :])
                    step(last)
                    dve.wait_ge(lg_exp, c + 1)
                    dve.memset(top[:, :, TOPK:8], -BIG).then_inc(top_done, 1)
                    dve.wait_ge(small_in, 64)
                    dve.wait_ge(top_done, c + 1)
                    for t in range(NT):
                        last = dve.match_replace(found[:, t, :], top[:, t, :], masked[:, t, :], BIG)
                    step(last)
                    step(dve.scalar_tensor_tensor(by_tile(w), found[:, :, 0:NE], BIG, by_tile(score), ALU.is_ge, ALU.mult))
                    tot = rg[:, 0, 0:NT]
                    step(dve.tensor_reduce(tot, by_tile(w), AX_X, ALU.add))
                    step(dve.tensor_scalar(tot, tot, 1e-20, None, ALU.add))
                    step(dve.reciprocal(tot, tot))
                    step(dve.scalar_tensor_tensor(comb[:, :, 0:NE], by_tile(w), ROUTE_SCALE, bc(tot, NE), ALU.mult, ALU.mult))

            def expert(c, u, following, first=False):
                for n, cn in gap_steps(u, 0, c, following, first):
                    prefix(n, whole(cn))
                dve.wait_ge(silu, c * NU + u + 1)
                dve.wait_ge(u_mm, c * NU + u + 1)
                if u >= NBUF or not first:
                    dve.wait_ge(h_lo, c * NU + u - NBUF + 1)
                dve.tensor_tensor(h_s[:, u % NBUF, :], sg[:, :], pu[:, u % 2, :], ALU.mult).then_inc(gated, 1)
                dve.wait_ge(gated, c * NU + u + 1)
                if u < NSH:
                    dve.sem_inc(weighted, 1)
                else:
                    dve.wait_ge(wts_in[u % 2], c * (NE * 8) + (u - NSH) // 2 * 16 + 16)
                    dve.tensor_tensor(h_s[:, u % NBUF, :], h_s[:, u % NBUF, :], wts[:, u % 2, :], ALU.mult).then_inc(weighted, 1)
                for n, cn in gap_steps(u, 1, c, following, first):
                    prefix(n, whole(cn))

            dve.memset(rstd[:, 3, :], EPS)
            dve.memset(masked[:, :, NE:NE + 8], -BIG)
            dve.memset(comb[:, :, NE:Q], 0.0)
            dve.memset(rstd[:, 1, :], -0.5).then_inc(consts, 1)
            dve.memset(rw_hl[:, :, :].bitcast(F32), 0.0).then_inc(consts, 1)
            dve.wait_ge(small_in, 64)
            dve.tensor_scalar(bq_s[:, :], col[:, C_BQ:C_BQ + KD], SCALE, None, ALU.mult)
            dve.tensor_scalar(bk_e[:, :], col[:, C_BK:C_BK + KD], even, None, ALU.mult).then_inc(consts, 1)
            for s, x in alone():
                if s in (3, 4) and not x.t0:
                    dve.wait_ge(aw_h_done, 1)
                    w = slice(0, W_K) if s == 3 else slice(W_K, W_R)
                    dve.tensor_tensor(aw_l[:, w], aw_s[:, w], aw_h[:, w].bitcast(F32), ALU.subtract).then_inc(aw_l_done, 1)
                if s == 7 and not x.t0:
                    r = aw_s[:, W_R:W_END].rearrange("p (k e) -> p k e", k=KD)
                    dve.wait_ge(consts, 3)
                    dve.tensor_copy(rw_hl[:, :, 0:NE], r).then_inc(consts, 1)
                    dve.wait_ge(consts, 4)
                    dve.tensor_tensor(rw_hl[:, :, NE:2 * NE], r, rw_hl[:, :, 0:NE].bitcast(F32), ALU.subtract).then_inc(rw_done, 1)
                prefix(s, x)
            for u in range(NU):
                expert(0, u, 1, first=True)
            with dve.Fori(1, NCH - 1) as c:
                for u in range(NU):
                    expert(c, u, c + 1)
            for u in range(NU):
                expert(NCH - 1, u, None)

        @block.gpsimd
        def _(pool):
            def rsqrt(i, v, tiles):
                pool.wait_ge(ln_mv[i], v + 1)
                pool.tensor_tensor(rstd[:, 0, tiles], mv[:, tiles, 1], rstd[:, 3, tiles], ALU.add).then_inc(ln_var[i], 1)
                pool.wait_ge(ln_var[i], v + 1)
                pool.tensor_tensor(rstd[:, 2, tiles], rstd[:, 0, tiles], rstd[:, 1, tiles], ALU.pow).then_inc(ln_rs[i], 1)

            def prefix(s, x):
                c, v, t0, nt, first = x
                cols, tiles = slice(t0 * P, (t0 + nt) * P), slice(t0, t0 + nt)
                if s == 1:
                    rsqrt(0, v, tiles)
                if s == 3:
                    pool.wait_ge(ln_xn[0], v + 1)
                    pool.tensor_tensor(hres[:, tiles, :], hres[:, tiles, :], row[:, D:2 * D].unsqueeze(1).to_broadcast([P, nt, D]), ALU.add)\
                        .then_inc(h0_bo, 1)
                if s in (10, 14):
                    m = int(s == 14)
                    half = these(m, x)
                    pool.wait_ge(sm_r01[m], v + 1)
                    pool.tensor_tensor(p32[:, half, SEQ:Q], sd[:, half, :], bc(rc[:, 2, half], SEQ), ALU.mult).then_inc(p_odd[m], 1)
                if s == 18:
                    rsqrt(1, v, tiles)

            def expert(c, u, following, first=False):
                for n, cn in gap_steps(u, 0, c, following, first):
                    prefix(n, whole(cn))
                pool.wait_ge(h_hi, c * NU + u + 1)
                if u >= NBUF or not first:
                    pool.wait_ge(down, c * NU + u - NBUF + 1)
                pool.tensor_tensor(hl[:, u % NBUF, :], h_s[:, u % NBUF, :], hh[:, u % NBUF, :].bitcast(F32), ALU.subtract).then_inc(h_lo, 1)
                for n, cn in gap_steps(u, 1, c, following, first):
                    prefix(n, whole(cn))

            def split_low(u):
                pool.wait_ge(fw_h_done, u + 1)
                pool.tensor_tensor(ffn_l[:, u, :], stage(u), ffn_h[:, u, :].bitcast(F32), ALU.subtract).then_inc(fw_l_done, 1)

            pool.wait_ge(consts, 1)
            pool.wait_ge(small_in, 64)
            for s, x in alone():
                for u in splits(SPLIT_LOW, s, x):
                    split_low(u)
                prefix(s, x)
            pool.wait_ge(fw_l_done, NU)
            for u in range(NU):
                expert(0, u, 1, first=True)
            with pool.Fori(1, NCH - 1) as c:
                for u in range(NU):
                    expert(c, u, c + 1)
            for u in range(NU):
                expert(NCH - 1, u, None)


def kernel(**inputs):
    import numpy as np
    import concourse.bacc as bacc
    from concourse.bass_utils import run_bass_kernel_spmd

    g = {k: np.asarray(v) for k, v in inputs.items()}
    C, F, PER = g["L0_tok_conv_w"].shape
    x = g["x"].reshape(TOK, PER, C).transpose(2, 1, 0).reshape(P, TOK)
    emb = g["L0_tok_emb_w"].T.reshape(C // 2, P, D).transpose(1, 0, 2).reshape(P, -1)
    conv = np.zeros((P, C // 2, 2, PER), np.float32)
    for ch in range(C):
        conv[(ch % 2) * F:(ch % 2) * F + F, ch // 2, ch % 2] = g["L0_tok_conv_w"][ch]
    tok = np.concatenate([emb, conv.reshape(P, -1)], 1)

    def halves(w):
        return w.reshape(KD, P, -1).transpose(1, 0, 2).reshape(P, -1)

    twice = lambda a, axis: np.concatenate([a, a], axis)
    attn = np.concatenate([halves(g["L0_attn_Wq"]), halves(twice(g["L0_attn_Wl"], 1)), twice(g["L0_attn_Wk"], 0),
                           twice(g["L0_attn_Wv"], 0), halves(g["L0_attn_Wo"]), halves(g["L0_ffn_router_weight"].T)], 1)
    experts = []
    for e in range(NSH):
        s = slice(e * P, e * P + P)
        experts.append((g["L0_ffn_sh_gate_w"][s], g["L0_ffn_sh_up_w"][s], g["L0_ffn_sh_down_w"][:, s]))
    for e in range(NE):
        experts.append((g["L0_ffn_gate_w"][e], g["L0_ffn_up_w"][e], g["L0_ffn_down_w"][e]))
    ffn = np.stack([np.concatenate([halves(a.T), halves(b.T), d.T], 1) for a, b, d in experts])
    half = (np.arange(P) // SEQ) % 2
    cols = np.concatenate([g["L0_attn_bq"].reshape(KD, P).T, twice(g["L0_attn_bl"], 0)[:, None], g["L0_attn_bk"].reshape(KD, P).T,
                           g["L0_attn_bv"].reshape(KD, P).T, (half == 0)[:, None], (half == 1)[:, None]], 1)
    rows = np.concatenate([g["L0_tok_emb_b"], g["L0_attn_bo"], g["L0_ffn_e_bias"]])
    tri = np.tril(np.ones((NGRP, NGRP)), -1).ravel()
    arrays = {"x_t": x, "tok_w": tok, "attn_w": attn, "ffn_w": ffn, "cols": cols, "rows": np.broadcast_to(rows, (P, rows.size)),
              "tri": np.broadcast_to(tri, (P, tri.size)), "ident": np.eye(P)}
    arrays = {k: np.ascontiguousarray(a, dtype=np.float32) for k, a in arrays.items()}

    nc = bacc.Bacc("TRN2", target_bir_lowering=False, num_devices=1)
    args = [nc.dram_tensor(n, a.shape, F32, kind="ExternalInput").ap() for n, a in arrays.items()]
    out = nc.dram_tensor("out_t", (D, TOK), F32, kind="ExternalOutput").ap()
    comb_d = nc.dram_tensor("comb_d", (NE, CH), F32, kind="Internal").ap()
    tower(nc, *args, out.rearrange("(k p) n -> p k n", p=P), comb_d)
    r = run_bass_kernel_spmd(nc, [arrays], core_ids=[0])
    return np.ascontiguousarray(r.results[0]["out_t"].T).reshape(TOK // SEQ, SEQ, D)
```
